# Optimizing a Trainium2 kernel written in Bass

```python
import numpy as np
import jax
import jax.numpy as jnp

def _softmax(x, axis=-1):
    return jax.nn.softmax(x, axis=axis)

def _gelu(x):
    return jax.nn.gelu(x, approximate=True)

def _silu(x):
    return jax.nn.silu(x)

def _sigmoid(x):
    return jax.nn.sigmoid(x)

def _layernorm(x, axis=-1, eps=1e-05):
    m = jnp.mean(x, axis=axis, keepdims=True)
    v = jnp.var(x, axis=axis, keepdims=True)
    return (x - m) / jnp.sqrt(v + eps)

def _scatter_add(tgt, idx, src, axis=0):
    return tgt.at[idx].add(src)

def _segment_sum(src, seg, n):
    return jax.ops.segment_sum(src, seg, n)
kernel_name = 'mk_gnn_resnorm_d2_gnn_r64_80a96d'

def setup_inputs(seed: int=0):
    np.random.seed(seed)
    _w = jnp.asarray

    def _rec_inputs():
        import jax
        import jax.numpy as jnp
        _gk = jax.random.key(seed)
        x = -0.0005121 + 1.001 * jax.random.normal(jax.random.fold_in(_gk, 1), (100000, 64), jnp.float32)
        src = jax.random.randint(jax.random.fold_in(_gk, 2), (25000,), 0, 100000, jnp.int32)
        dst = jnp.minimum((100000 * jax.random.uniform(jax.random.fold_in(_gk, 3), (25000,)) ** 2.0).astype(jnp.int32), 99999)
        _o = jnp.argsort(dst, stable=True)
        src = src[_o]
        dst = dst[_o]
        edge_attr_64 = -2.25437e-05 + 0.999858 * jax.random.normal(jax.random.fold_in(_gk, 12), (25000, 64), jnp.float32)
        edge_weight = jax.random.uniform(jax.random.fold_in(_gk, 14), (25000,), jnp.float32, 0.0, 0.999998)
        node_vec1 = jax.random.uniform(jax.random.fold_in(_gk, 15), (100000, 1), jnp.float32, 0.0, 0.999993)
        node_vec1_n2 = jax.random.uniform(jax.random.fold_in(_gk, 16), (100000, 1), jnp.float32, 0.0, 0.999993)
        return (x, src, dst, edge_attr_64, edge_weight, node_vec1, node_vec1_n2)
    x, src, dst, edge_attr_64, edge_weight, node_vec1, node_vec1_n2 = _rec_inputs()

    def _L0_gnn_setup():
        import jax, jax.numpy as jnp
        import numpy as np
        N, E = (50000, 1250000)
        IN_DIM, OUT_DIM, HEADS = (64, 64, 4)
        NEG_SLOPE = 0.2
        LN_EPS = 1e-05
        SM_EPS = 1e-16

        def _gat_conv(x, src, dst, W, a_src, a_dst, b, heads, out_c, concat):
            n = x.shape[0]
            xw = (x @ W).reshape(n, heads, out_c)
            asrc = jnp.einsum('nhc,hc->nh', xw, a_src)
            adst = jnp.einsum('nhc,hc->nh', xw, a_dst)
            loop = jnp.arange(n, dtype=src.dtype)
            s = jnp.concatenate([src, loop])
            d = jnp.concatenate([dst, loop])
            e = jax.nn.leaky_relu(asrc[s] + adst[d], NEG_SLOPE)
            m = jax.ops.segment_max(e, d, num_segments=n)
            ex = jnp.exp(e - m[d])
            denom = jax.ops.segment_sum(ex, d, num_segments=n)
            att = ex / (denom[d] + SM_EPS)
            msg = xw[s] * att[:, :, None]
            out = jax.ops.segment_sum(msg, d, num_segments=n)
            out = out.reshape(n, heads * out_c) if concat else out.mean(axis=1)
            return out + b

        def _layer_norm(x, g, b):
            mu = x.mean(-1, keepdims=True)
            var = ((x - mu) ** 2).mean(-1, keepdims=True)
            return (x - mu) * jax.lax.rsqrt(var + LN_EPS) * g + b
        key = jax.random.key(seed)
        ks = jax.random.split(key, 12)
        s = 0.1
        return {'h': jax.random.normal(ks[0], (N, IN_DIM), jnp.float32), 'edge_index': jax.random.randint(ks[1], (2, E), 0, N, jnp.int32), 'W1': jax.random.normal(ks[2], (IN_DIM, HEADS * 16), jnp.float32) * s, 'a1_src': jax.random.normal(ks[3], (HEADS, 16), jnp.float32) * s, 'a1_dst': jax.random.normal(ks[4], (HEADS, 16), jnp.float32) * s, 'b1': jnp.zeros((HEADS * 16,), jnp.float32), 'W2': jax.random.normal(ks[5], (OUT_DIM, OUT_DIM), jnp.float32) * s, 'a2_src': jax.random.normal(ks[6], (1, OUT_DIM), jnp.float32) * s, 'a2_dst': jax.random.normal(ks[7], (1, OUT_DIM), jnp.float32) * s, 'b2': jnp.zeros((OUT_DIM,), jnp.float32), 'ln1_g': jnp.ones((OUT_DIM,), jnp.float32), 'ln1_b': jnp.zeros((OUT_DIM,), jnp.float32), 'ln2_g': jnp.ones((OUT_DIM,), jnp.float32), 'ln2_b': jnp.zeros((OUT_DIM,), jnp.float32)}
    _L0_gnn_all = _L0_gnn_setup()
    _L0_gnn_in = {k: v for k, v in _L0_gnn_all.items() if k in ('W1', 'a1_src', 'a1_dst', 'b1', 'W2', 'a2_src', 'a2_dst', 'b2', 'ln1_g', 'ln1_b', 'ln2_g', 'ln2_b')}
    del _L0_gnn_all

    def _L1_gnn_setup():
        import jax, jax.numpy as jnp
        import numpy as np
        N_SRC = 100000
        N_DST = 100000
        E = 15625
        D = 64
        key = jax.random.key(seed)
        ks = jax.random.split(key, 10)
        return {'weight': jax.random.normal(ks[0], (N_SRC, D), jnp.float32) * 0.02, 'review_feat': jax.random.normal(ks[1], (E, D), jnp.float32), 'attn': jax.random.uniform(ks[2], (E,), jnp.float32), 'cj': jax.random.uniform(ks[3], (N_SRC, 1), jnp.float32), 'ci': jax.random.uniform(ks[4], (N_DST, 1), jnp.float32), 'prob_w': jax.random.normal(ks[5], (1, D), jnp.float32) * 0.1, 'review_score_w': jax.random.normal(ks[6], (1, D), jnp.float32) * 0.1, 'review_w': jax.random.normal(ks[7], (D, D), jnp.float32) * 0.1, 'src_idx': jax.random.randint(ks[8], (E,), 0, N_SRC, jnp.int32), 'dst_idx': jax.random.randint(ks[9], (E,), 0, N_DST, jnp.int32)}
    _L1_gnn_all = _L1_gnn_setup()
    _L1_gnn_in = {k: v for k, v in _L1_gnn_all.items() if k in ('prob_w', 'review_score_w', 'review_w')}
    del _L1_gnn_all
    return {'x': x, 'src': src, 'dst': dst, 'edge_attr_64': edge_attr_64, 'edge_weight': edge_weight, 'node_vec1': node_vec1, 'node_vec1_n2': node_vec1_n2, 'L0_gnn_W1': _L0_gnn_in['W1'], 'L0_gnn_a1_src': _L0_gnn_in['a1_src'], 'L0_gnn_a1_dst': _L0_gnn_in['a1_dst'], 'L0_gnn_b1': _L0_gnn_in['b1'], 'L0_gnn_W2': _L0_gnn_in['W2'], 'L0_gnn_a2_src': _L0_gnn_in['a2_src'], 'L0_gnn_a2_dst': _L0_gnn_in['a2_dst'], 'L0_gnn_b2': _L0_gnn_in['b2'], 'L0_gnn_ln1_g': _L0_gnn_in['ln1_g'], 'L0_gnn_ln1_b': _L0_gnn_in['ln1_b'], 'L0_gnn_ln2_g': _L0_gnn_in['ln2_g'], 'L0_gnn_ln2_b': _L0_gnn_in['ln2_b'], 'L1_gnn_prob_w': _L1_gnn_in['prob_w'], 'L1_gnn_review_score_w': _L1_gnn_in['review_score_w'], 'L1_gnn_review_w': _L1_gnn_in['review_w']}

def reference(x, src, dst, edge_attr_64, edge_weight, node_vec1, node_vec1_n2, L0_gnn_W1, L0_gnn_a1_src, L0_gnn_a1_dst, L0_gnn_b1, L0_gnn_W2, L0_gnn_a2_src, L0_gnn_a2_dst, L0_gnn_b2, L0_gnn_ln1_g, L0_gnn_ln1_b, L0_gnn_ln2_g, L0_gnn_ln2_b, L1_gnn_prob_w, L1_gnn_review_score_w, L1_gnn_review_w):
    import jax
    import jax.numpy as jnp

    def _L0_gnn_ref(h, edge_index, W1, a1_src, a1_dst, b1, W2, a2_src, a2_dst, b2, ln1_g, ln1_b, ln2_g, ln2_b):
        import jax, jax.numpy as jnp
        import numpy as np
        N, E = (50000, 1250000)
        IN_DIM, OUT_DIM, HEADS = (64, 64, 4)
        NEG_SLOPE = 0.2
        LN_EPS = 1e-05
        SM_EPS = 1e-16

        def _gat_conv(x, src, dst, W, a_src, a_dst, b, heads, out_c, concat):
            n = x.shape[0]
            xw = (x @ W).reshape(n, heads, out_c)
            asrc = jnp.einsum('nhc,hc->nh', xw, a_src)
            adst = jnp.einsum('nhc,hc->nh', xw, a_dst)
            loop = jnp.arange(n, dtype=src.dtype)
            s = jnp.concatenate([src, loop])
            d = jnp.concatenate([dst, loop])
            e = jax.nn.leaky_relu(asrc[s] + adst[d], NEG_SLOPE)
            m = jax.ops.segment_max(e, d, num_segments=n)
            ex = jnp.exp(e - m[d])
            denom = jax.ops.segment_sum(ex, d, num_segments=n)
            att = ex / (denom[d] + SM_EPS)
            msg = xw[s] * att[:, :, None]
            out = jax.ops.segment_sum(msg, d, num_segments=n)
            out = out.reshape(n, heads * out_c) if concat else out.mean(axis=1)
            return out + b

        def _layer_norm(x, g, b):
            mu = x.mean(-1, keepdims=True)
            var = ((x - mu) ** 2).mean(-1, keepdims=True)
            return (x - mu) * jax.lax.rsqrt(var + LN_EPS) * g + b
        src, dst = (edge_index[0], edge_index[1])
        x = _gat_conv(h, src, dst, W1, a1_src, a1_dst, b1, HEADS, 16, True)
        x = jax.nn.elu(_layer_norm(x, ln1_g, ln1_b))
        z = _gat_conv(x, src, dst, W2, a2_src, a2_dst, b2, 1, OUT_DIM, False)
        z = jax.nn.elu(_layer_norm(z, ln2_g, ln2_b))
        return z

    def _L1_gnn_ref(weight, review_feat, attn, cj, ci, prob_w, review_score_w, review_w, src_idx, dst_idx):
        import jax, jax.numpy as jnp
        import numpy as np
        N_SRC = 100000
        N_DST = 100000
        E = 15625
        D = 64
        pa = jax.nn.sigmoid(review_feat @ prob_w.T)
        ra = jax.nn.sigmoid(review_feat @ review_score_w.T)
        rf = review_feat @ review_w.T
        h_src = weight[src_idx]
        cj_e = cj[src_idx]
        a = attn[:, None]
        m = (h_src * pa + rf * (ra * a)) * cj_e
        h = jax.ops.segment_sum(m, dst_idx, num_segments=ci.shape[0])
        return h * ci
    edge_index = jnp.stack([src, dst])
    x = _layernorm(x + _L0_gnn_ref(x, edge_index, L0_gnn_W1, L0_gnn_a1_src, L0_gnn_a1_dst, L0_gnn_b1, L0_gnn_W2, L0_gnn_a2_src, L0_gnn_a2_dst, L0_gnn_b2, L0_gnn_ln1_g, L0_gnn_ln1_b, L0_gnn_ln2_g, L0_gnn_ln2_b), axis=-1)
    x = _layernorm(x + _L1_gnn_ref(x, edge_attr_64, edge_weight, node_vec1, node_vec1_n2, L1_gnn_prob_w, L1_gnn_review_score_w, L1_gnn_review_w, src, dst), axis=-1)
    return x

_drawn_inputs = setup_inputs


def setup_inputs(seed=0):
    import zlib

    import numpy as np

    out = dict(_drawn_inputs(seed))
    spreads = {'L0_gnn_b1': (0.0, 0.1),
     'L0_gnn_b2': (0.0, 0.1),
     'L0_gnn_ln1_g': (1.0, 0.2),
     'L0_gnn_ln1_b': (0.0, 0.1),
     'L0_gnn_ln2_g': (1.0, 0.2),
     'L0_gnn_ln2_b': (0.0, 0.1)}
    factors = {'edge_weight': 3.332,
     'L0_gnn_a1_dst': 4.694,
     'L0_gnn_a2_dst': 5.304,
     'L1_gnn_review_score_w': 4.406}
    for name, (base, spread) in spreads.items():
        noise = np.random.default_rng([zlib.crc32(name.encode()), seed]).standard_normal(out[name].shape)
        drawn = base * np.exp(spread * noise) if base else spread * noise
        out[name] = jnp.asarray(drawn.astype(out[name].dtype))
    for name, factor in factors.items():
        out[name] = (out[name] * factor).astype(out[name].dtype)
    return out
```

```python
from contextlib import ExitStack

import concourse.bass as bass
from concourse import mybir

ALU = mybir.AluOpType
ACT = mybir.ActivationFunctionType
AX = mybir.AxisListType
F32 = mybir.dt.float32
I32 = mybir.dt.int32

P = 128
C = 64
HEADS = 4
N, E = 100000, 25000
ROW = C + 1
CH = 8
UNIT = P * CH
TILES = -(-E // (4 * P)) * 4
EP = TILES * P
STEPS = TILES // 4
NP = 2 * STEPS * UNIT
assert NP > N and STEPS % 2 == 1
RQ = EP // 256
LAG = 2
BIG = 1.0e30
SKIP = 1 << 20
LN_EPS = 1e-5
SM_EPS = 1e-16
SLOPE = 0.2

COLS = {}
WIDTH = 0
for _name, _w in (("ident", P), ("cbd", P), ("jbd", P), ("clo", P), ("chi", P), ("w1t", P), ("w1", P), ("al1", 8),
                  ("al2", 8), ("w2t", P), ("w2", P), ("sel2", 132), ("rev", 132), ("vec", 10)):
    COLS[_name] = (WIDTH, WIDTH + _w)
    WIDTH += _w
B1, B2, G1, BE1, G2, BE2, ONE, EPS, EPS2, ZERO = range(10)


def after(eng, sem, count):
    if isinstance(count, int) and count <= 0:
        return
    eng.wait_ge(sem, count)


def after_apart(eng, sem, count, s_passed):
    after(eng, sem, count)
    if not isinstance(count, int):
        eng.sem_inc(s_passed, 1)


class Step:

    def __init__(self, k, half, odd):
        self.k, self.half, self.odd = k, half, odd

    def back(self, n):
        k = self.k - n
        if isinstance(k, int):
            return Step(k, k // 2, k % 2)
        return Step(k, self.half + (self.odd - n) // 2, (self.odd - n) % 2)

    def runs(self):
        return not isinstance(self.k, int) or 0 <= self.k < STEPS


def run_steps(eng, body, lag=LAG):
    for k in range(4):
        body(Step(k, k // 2, k % 2))
    with eng.Fori(2, STEPS // 2) as m:
        body(Step(2 * m, m, 0))
        body(Step(2 * m + 1, m, 1))
    for k in range(STEPS - 1, STEPS + lag):
        body(Step(k, k // 2, k % 2))


class Shared:
    pass


def gnn_program(nc, x, xs, xt, src, dst, ew, ea, wts_in, out):
    ctx = ExitStack()

    def sb(name, shape, dt=F32, on=ctx):
        return on.enter_context(nc.sbuf_tensor(name, shape, dt))

    def scratch(name, shape, dt=F32):
        return nc.dram_tensor(name, shape, dt, kind="Internal").ap()

    y_table = scratch("y_table", (NP, C))
    x1_table = scratch("x1_table", (NP, C))
    dst_s = scratch("dst_s", (EP + 2,), I32)
    src_s = scratch("src_s", (EP,), I32)
    ew_s = scratch("ew_s", (EP,))
    ea_s = scratch("ea_s", (EP, C))
    same_d = scratch("same_d", (EP,))
    xd_d = scratch("xd_d", (P, TILES, C))

    with ctx:
        bank = [ctx.enter_context(nc.psum_tensor(f"bank{i}", [P, 512], F32)) for i in range(8)]
        wts = sb("wts", [P, WIDTH])
        w1c = sb("w1c", [P, P])
        w2c = sb("w2c", [P, P])
        r2 = sb("r2", [P, 132])
        lgw = sb("lgw", [P, 8])
        col = sb("col", [P, 6])
        srci = sb("srci", [P, TILES], I32)
        dsti = sb("dsti", [P, TILES], I32)
        lasti = sb("lasti", [P, TILES], I32)
        ewp = sb("ewp", [P, TILES])
        cjp = sb("cjp", [P, TILES])
        cip = sb("cip", [P, TILES])
        lg = sb("lg", [P, TILES, 8])
        att = sb("att", [P, TILES, 8])
        same = sb("same", [RQ, 256])
        fresh = sb("fresh", [RQ, 256])
        more = sb("more", [RQ, 256])
        last = sb("last", [RQ, 256])
        pre = sb("pre", [RQ, 256])
        prefresh = sb("prefresh", [RQ, 256])
        suf = sb("suf", [RQ, 256])
        tmask = sb("tmask", [HEADS, 3, RQ])

        def w(name, rows=P):
            a, b = COLS[name]
            return wts[0:rows, a:b]

        def vec(i):
            return wts[:, COLS["vec"][0] + i:COLS["vec"][0] + i + 1]

        ident = w("ident")
        b1c, b2c, b2c_dense, be1p, be2p = (col[:, i:i + 1] for i in range(5))

        phase_sems = []

        ended = []

        def sem(name):
            s = nc.alloc_semaphore(f"{name}_{len(ended)}")
            phase_sems.append(s)
            return s

        def end_phase():
            nc.clear_and_free_semaphores(list(phase_sems))
            phase_sems.clear()
            ended.append(len(ended))
            nc.all_engine_barrier()

        v = Shared()
        v.x, v.xs, v.xt, v.dst, v.src, v.ew, v.ea, v.wts_in, v.out = x, xs, xt, dst, src, ew, ea, wts_in, out
        v.y_table, v.x1_table, v.dst_s, v.src_s, v.ew_s, v.ea_s, v.same_d, v.xd_d = (
            y_table, x1_table, dst_s, src_s, ew_s, ea_s, same_d, xd_d)
        v.bank, v.wts, v.vec, v.ident, v.w1c, v.w2c, v.r2, v.lgw = bank, wts, vec, ident, w1c, w2c, r2, lgw
        v.b1c, v.b2c, v.b2c_dense, v.be1p, v.be2p = b1c, b2c, b2c_dense, be1p, be2p
        v.srci, v.dsti, v.lasti, v.ewp, v.cjp, v.cip, v.lg, v.att = srci, dsti, lasti, ewp, cjp, cip, lg, att
        v.same, v.fresh, v.more, v.last, v.pre, v.prefresh, v.suf, v.tmask = (
            same, fresh, more, last, pre, prefresh, suf, tmask)
        v.s_passed = nc.alloc_semaphore("s_passed")
        s_reviews = nc.alloc_semaphore("s_reviews")

        sort_edges(nc, sb, sem, end_phase, v, s_reviews)

        with ExitStack() as ph:
            dc = sb("dc", [RQ, 3, 256], I32, ph)
            df = sb("df", [RQ, 3, 256], F32, ph)
            sc = sb("sc", [RQ, 2, 256], I32, ph)
            turn = sb("turn", [RQ, 4, 256], F32, ph)
            ends = sb("ends", [RQ, 3, HEADS], F32, ph)
            bcol = sb("bcol", [P, 1], F32, ph)
            s_ld = [sem(f"s_ld{i}") for i in range(5)]
            s_v = sem("s_v")
            s_turn = sem("s_turn")
            s_ends = sem("s_ends")
            s_col = sem("s_col")
            s_pt = sem("s_pt")
            s_pe = sem("s_pe")
            s_pw = sem("s_pw")
            s_pb = sem("s_pb")
            s_same = sem("s_same")
            s_st = sem("s_st")
            block = nc.Block()
            with block:
                @block.sync
                def _(sp):
                    for n in range(3):
                        o = (1, 0, 2)[n]
                        sp.dma_start(dc[:, n, :], dst_s[o:o + EP].rearrange("(q j) -> q j", j=256)).then_inc(s_ld[n], 16)
                    sp.dma_start(sc[:, 0, :], src_s.rearrange("(q j) -> q j", j=256)).then_inc(s_ld[3], 16)
                    sp.dma_start(turn[:, 3, :], ew_s.rearrange("(q j) -> q j", j=256)).then_inc(s_ld[4], 16)
                    sp.wait_ge(s_same, 1)
                    sp.dma_start(same_d.rearrange("(q j) -> q j", j=256), same[:, :]).then_inc(s_st, 16)
                    sp.wait_ge(s_st, 16)

                @block.vector
                def _(dve):
                    chain = [0]

                    def link(ins):
                        chain[0] += 1
                        ins.then_inc(s_v, 1)
                        dve.wait_ge(s_v, chain[0])

                    for n in range(3):
                        dve.wait_ge(s_ld[n], 16)
                    link(nc.vector.tensor_copy(df[:, :, :], dc[:, :, :]))
                    link(nc.vector.tensor_tensor(same[:, :], df[:, 0, :], df[:, 1, :], ALU.is_equal))
                    nc.vector.tensor_tensor(more[:, :], df[:, 0, :], df[:, 2, :], ALU.is_equal).then_inc(s_same, 1)
                    dve.wait_ge(s_same, 1)
                    link(nc.vector.tensor_scalar(fresh[:, :], same[:, :], -1.0, BIG, ALU.add, ALU.mult))
                    link(nc.vector.tensor_scalar(last[:, :], more[:, :], -1.0, 1.0, ALU.mult, ALU.add))
                    link(nc.vector.tensor_tensor_scan(pre[:, :], same[:, :], same[:, :], 1.0, ALU.mult, ALU.min))
                    link(nc.vector.tensor_tensor_scan(suf[:, ::-1], more[:, ::-1], more[:, ::-1], 1.0, ALU.mult, ALU.min))
                    link(nc.vector.tensor_scalar(prefresh[:, :], pre[:, :], -1.0, BIG, ALU.add, ALU.mult))
                    dve.wait_ge(s_ld[3], 16)
                    link(nc.vector.tensor_copy(turn[:, 0, :], sc[:, 0, :]))
                    link(nc.vector.tensor_copy(turn[:, 1, :], df[:, 0, :]))
                    nc.vector.scalar_tensor_tensor(out=turn[:, 2, :], in0=more[:, :], scalar=float(SKIP), in1=df[:, 0, :],
                                                   op0=ALU.mult, op1=ALU.add).then_inc(s_turn, 1)
                    for i, m in enumerate((pre[:, 255:256], prefresh[:, 255:256], suf[:, 0:1])):
                        z = nc.vector.tensor_copy(ends[:, i, :], m.to_broadcast([RQ, HEADS]))
                    z.then_inc(s_ends, 1)
                    dve.wait_ge(s_pt, 1)

                    def slots(n):
                        return bank[n // 2][:, (n % 2) * 256:(n % 2) * 256 + 2 * P].rearrange(
                            "p (s q) -> p s q", s=2)[:, :, 0:RQ]

                    for n, to in enumerate((srci, dsti, lasti, ewp)):
                        link(nc.vector.tensor_copy(to[:, :].rearrange("p (q s) -> p s q", s=2), slots(n)))
                    dve.wait_ge(s_pe, 1)
                    for i in range(3):
                        z = nc.vector.tensor_copy(tmask[:, i, :], bank[2][0:HEADS, i * P:i * P + RQ])
                    link(z)
                    dve.wait_ge(s_pw, 1)
                    nc.vector.tensor_copy(w1c[:, :], bank[3][:, 0:P])
                    nc.vector.tensor_copy(w2c[:, :], bank[3][:, P:2 * P])
                    nc.vector.tensor_copy(r2[:, :], bank[3][:, 2 * P:2 * P + 132])
                    nc.vector.tensor_copy(lgw[:, :], bank[4][:, 0:8])
                    nc.vector.tensor_copy(col[:, 0:2], bank[4][:, 8:10])
                    nc.vector.tensor_tensor(bcol[:, :], vec(B2), bank[4][:, 10:11], ALU.subtract).then_inc(s_col, 1)
                    nc.vector.tensor_scalar(col[:, 3:4], vec(BE1), 1.0, None, ALU.add)
                    nc.vector.tensor_scalar(col[:, 4:5], vec(BE2), 1.0, None, ALU.add)
                    dve.wait_ge(s_pb, 1)
                    link(nc.vector.tensor_copy(col[:, 2:3], bank[4][:, 12:13]))

                @block.tensor
                def _(pe):
                    pe.wait_ge(s_turn, 1)
                    pe.wait_ge(s_ld[4], 16)
                    for n in range(4):
                        for s in range(2):
                            z = nc.tensor.transpose(bank[n // 2][:, (n % 2) * 256 + s * P:(n % 2) * 256 + s * P + RQ],
                                                    turn[:, n, s * P:(s + 1) * P], ident[0:RQ, 0:RQ])
                    z.then_inc(s_pt, 1)
                    pe.wait_ge(s_ends, 1)
                    for i in range(3):
                        z = nc.tensor.transpose(bank[2][0:HEADS, i * P:i * P + RQ], ends[:, i, :], ident[0:RQ, 0:RQ])
                    z.then_inc(s_pe, 1)
                    nc.tensor.matmul(bank[3][:, 0:P], w("w1t"), w("cbd"), start=True, stop=True)
                    nc.tensor.matmul(bank[3][:, P:2 * P], w("w2t"), w("cbd"), start=True, stop=True)
                    nc.tensor.matmul(bank[3][:, 2 * P:2 * P + 132], w("w2t"), w("sel2"), start=True, stop=True)
                    nc.tensor.matmul(bank[4][:, 0:8], w("w1t"), w("al1"), start=True, stop=False)
                    nc.tensor.matmul(bank[4][:, 0:8], w("w1t"), w("al2"), start=False, stop=True)
                    nc.tensor.matmul(bank[4][:, 8:10], w("cbd"), w("vec")[:, B1:B2 + 1], start=True, stop=True)
                    nc.tensor.matmul(bank[4][:, 10:11], w("w2"), vec(ONE), start=True, stop=True).then_inc(s_pw, 1)
                    pe.wait_ge(s_col, 1)
                    nc.tensor.matmul(bank[4][:, 12:13], w("cbd"), bcol[:, :], start=True, stop=True).then_inc(s_pb, 1)
            end_phase()

        v.xw = sb("xw", [P, TILES, 2 * C])
        dense_and_gather(nc, sb, sem, bank, w, vec, v)
        end_phase()
        softmax(nc, sb, sem, bank, v, 1)
        end_phase()
        aggregate1(nc, sb, sem, bank, w, vec, v)
        end_phase()
        v.adc = sb("adc", [RQ, 2, 256])
        gather2(nc, sb, sem, bank, w, vec, v)
        end_phase()
        softmax(nc, sb, sem, bank, v, 2)
        end_phase()
        v.x1r = v.xw[:, :, 0:C]
        aggregate2(nc, sb, sem, bank, w, vec, v)
        end_phase()
        aggregate3(nc, sb, sem, bank, w, vec, v, s_reviews)
        end_phase()


def sort_edges(nc, sb0, sem, end_phase, v, s_reviews):
    CHUNK = EP // 7
    with ExitStack() as ph:
        cur = sb0("s_cur", [RQ, 2, 256], I32, ph)
        curf = sb0("s_curf", [RQ, 2, 256], F32, ph)
        down = sb0("s_down", [RQ, 1], F32, ph)
        flag = sb0("s_flag", [1, 1], I32, ph)
        s_ld, s_wt, s_c, s_dn, s_sum, s_flag = [sem(n) for n in "s_ld s_wt s_c s_dn s_sum s_flag".split()]
        with nc.Block() as block:
            @block.sync
            def _(sp):
                sp.dma_start(cur[:, 0, :], v.dst[1:1 + EP].rearrange("(q j) -> q j", j=256)).then_inc(s_ld, 16)
                sp.dma_start(cur[:, 1, :], v.dst[2:2 + EP].rearrange("(q j) -> q j", j=256)).then_inc(s_ld, 16)
                sp.dma_start(v.wts[:, :], v.wts_in).then_inc(s_wt, 16)
                sp.wait_ge(s_flag, 1)

            @block.vector
            def _(dve):
                dve.wait_ge(s_ld, 32)
                nc.vector.tensor_copy(curf[:, :, :], cur[:, :, :]).then_inc(s_c, 1)
                dve.wait_ge(s_c, 1)
                nc.vector.tensor_tensor(curf[:, 0, :], curf[:, 0, :], curf[:, 1, :], ALU.is_gt).then_inc(s_c, 1)
                dve.wait_ge(s_c, 2)
                nc.vector.tensor_reduce(down[:, :], curf[:, 0, :], AX.X, ALU.add).then_inc(s_dn, 1)
                dve.wait_ge(s_sum, 1)
                nc.vector.tensor_scalar(flag[:, :], v.bank[0][0:1, 0:1], 1.0, None, ALU.min).then_inc(s_flag, 1)

            @block.tensor
            def _(pe):
                pe.wait_ge(s_wt, 16)
                pe.wait_ge(s_dn, 1)
                nc.tensor.matmul(v.bank[0][0:1, 0:1], down[:, :], v.vec(ONE)[0:RQ, :], start=True, stop=True).then_inc(s_sum, 1)
        end_phase()

        kpi = sb0("s_kpi", [P, TILES], I32, ph)
        spi = sb0("s_spi", [P, TILES], I32, ph)
        epi = sb0("s_epi", [P, TILES], F32, ph)
        kpf = sb0("s_kpf", [P, TILES], F32, ph)
        ownf = sb0("s_ownf", [P, TILES], F32, ph)
        own = sb0("s_own", [P, TILES], I32, ph)
        part = sb0("s_part", [P, TILES], F32, ph)
        rank = sb0("s_rank", [P, TILES], F32, ph)
        ranki = sb0("s_ranki", [P, 2, TILES], I32, ph)
        rowi = sb0("s_rowi", [P, CHUNK], I32, ph)
        rowf = sb0("s_rowf", [P, CHUNK], F32, ph)
        numi = sb0("s_numi", [P, CHUNK], I32, ph)
        numf = sb0("s_numf", [P, CHUNK], F32, ph)
        less = sb0("s_less", [P, CHUNK], F32, ph)
        tie = sb0("s_tie", [P, CHUNK], F32, ph)
        stage = sb0("s_stage", [P, 4], I32, ph)
        stagef = sb0("s_stagef", [P, 1], F32, ph)
        stager = sb0("s_stager", [P, C], F32, ph)
        s_own, s_in, s_row, s_v, s_rank, s_stage, s_rv, s_all, s_cp, s_pad = [sem(n) for n in (
            "s_own s_in s_row s_v s_rank s_stage s_rv s_all s_cp s_pad").split()]
        s_put = [sem(f"s_put{n}") for n in range(4)]

        with nc.Block() as block:
            @block.sync
            def _(sp):
                unsorted = sp.value_load(flag[0:1, 0:1], min_val=0, max_val=1)
                with sp.If(unsorted == 0):
                    sp.dma_start(v.dst_s, v.dst).then_inc(s_cp, 16)
                    sp.dma_start(v.src_s, v.src).then_inc(s_cp, 16)
                    sp.dma_start(v.ew_s, v.ew).then_inc(s_cp, 16)
                    sp.dma_start(v.ea_s.rearrange("(a b) f -> a (b f)", a=P), v.ea.rearrange("(a b) f -> a (b f)", a=P)
                                 ).then_inc(s_reviews, 16)
                    sp.wait_ge(s_cp, 48)
                with sp.Else():
                    sp.dma_start(kpi[:, :], v.dst[1:1 + EP].rearrange("(p t) -> p t", t=TILES)).then_inc(s_in, 16)
                    sp.dma_start(spi[:, :], v.src.rearrange("(p t) -> p t", t=TILES)).then_inc(s_in, 16)
                    sp.dma_start(epi[:, :], v.ew.rearrange("(p t) -> p t", t=TILES)).then_inc(s_in, 16)
                    for c in range(EP // CHUNK):
                        after_apart(sp, s_v, 3 + c * (5 * TILES + 3), v.s_passed)
                        sp.dma_start(rowi[:, :], v.dst[1 + c * CHUNK:1 + (c + 1) * CHUNK].unsqueeze(0).to_broadcast([P, CHUNK])
                                     ).then_inc(s_row, 16)
                    sp.dma_start(v.dst_s[0:1], v.dst[0:1]).then_inc(s_pad, 16)
                    sp.dma_start(v.dst_s[EP + 1:EP + 2], v.dst[EP + 1:EP + 2]).then_inc(s_pad, 16)
                    sp.wait_ge(s_pad, 32)
                    sp.wait_ge(s_all, 1)
                    sp.dma_start(v.dst_s[0:1], v.dst[0:1]).then_inc(s_reviews, 16)

            @block.vector
            def _(dve):
                unsorted = dve.value_load(flag[0:1, 0:1], min_val=0, max_val=1)
                with dve.If(unsorted == 1):
                    dve.wait_ge(s_own, 1)
                    dve.wait_ge(s_in, 48)
                    nc.vector.tensor_copy(ownf[:, :], own[:, :])
                    nc.vector.tensor_copy(numf[:, :], numi[:, :]).then_inc(s_v, 1)
                    nc.vector.tensor_copy(kpf[:, :], kpi[:, :]).then_inc(s_v, 1)
                    nc.vector.memset(rank[:, :], 0.0).then_inc(s_v, 1)
                    for c in range(EP // CHUNK):
                        done = 3 + c * (5 * TILES + 3)
                        dve.wait_ge(s_v, done)
                        dve.wait_ge(s_row, 16 * (c + 1))
                        nc.vector.tensor_copy(rowf[:, :], rowi[:, :]).then_inc(s_v, 1)
                        with dve.Fori(0, TILES) as t:
                            one = bass.ds(t, 1)
                            dve.wait_ge(s_v, 5 * t + (done + 1))
                            nc.vector.tensor_scalar(less[:, :], rowf[:, :], kpf[:, one], None, ALU.is_lt).then_inc(s_v, 1)
                            nc.vector.tensor_scalar(tie[:, :], rowf[:, :], kpf[:, one], None, ALU.is_equal).then_inc(s_v, 1)
                            dve.wait_ge(s_v, 5 * t + (done + 3))
                            nc.vector.scalar_tensor_tensor(out=tie[:, :], in0=numf[:, :], scalar=ownf[:, one], in1=tie[:, :],
                                                           op0=ALU.is_lt, op1=ALU.mult).then_inc(s_v, 1)
                            dve.wait_ge(s_v, 5 * t + (done + 4))
                            nc.vector.tensor_tensor(less[:, :], less[:, :], tie[:, :], ALU.add).then_inc(s_v, 1)
                            dve.wait_ge(s_v, 5 * t + (done + 5))
                            nc.vector.tensor_reduce(part[:, one], less[:, :], AX.X, ALU.add).then_inc(s_v, 1)
                        dve.wait_ge(s_v, done + 1 + 5 * TILES)
                        nc.vector.tensor_scalar(numf[:, :], numf[:, :], float(CHUNK), None, ALU.add).then_inc(s_v, 1)
                        nc.vector.tensor_tensor(rank[:, :], rank[:, :], part[:, :], ALU.add).then_inc(s_v, 1)
                    dve.wait_ge(s_v, 3 + (EP // CHUNK) * (5 * TILES + 3))
                    nc.vector.tensor_copy(ranki[:, 0, :], rank[:, :])
                    nc.vector.tensor_scalar(ranki[:, 1, :], rank[:, :], 1.0, None, ALU.add).then_inc(s_rank, 1)
                with dve.Else():
                    dve.wait_ge(s_own, 1)

            @block.gpsimd
            def _(pool):
                unsorted = pool.value_load(flag[0:1, 0:1], min_val=0, max_val=1)
                pool.iota(own[:, :], pattern=[[1, TILES]], base=0, channel_multiplier=TILES)
                pool.iota(numi[:, :], pattern=[[1, CHUNK]], base=0, channel_multiplier=0).then_inc(s_own, 1)
                with pool.If(unsorted == 1):
                    pool.wait_ge(s_rank, 1)
                    pool.wait_ge(s_in, 48)
                    rows = v.ea.rearrange("(p t) f -> p t f", t=TILES)
                    with pool.Fori(0, TILES) as t:
                        one = bass.ds(t, 1)
                        nc.gpsimd.tensor_copy(stage[:, 0:2], ranki[:, :, one].rearrange("p a b -> p (a b)"))
                        nc.gpsimd.tensor_copy(stage[:, 2:3], kpi[:, one])
                        nc.gpsimd.tensor_copy(stage[:, 3:4], spi[:, one])
                        nc.gpsimd.tensor_copy(stagef[:, :], epi[:, one]).then_inc(s_stage, 1)
                        pool.dma_start(stager[:, :], rows[:, one, :].rearrange("p a f -> p (a f)")).then_inc(s_rv, 16)
                        pool.wait_ge(s_stage, t + 1)
                        after_apart(pool, s_rv, 16 * t + 16, v.s_passed)
                        for n, (to, at, val) in enumerate((
                                (v.src_s.unsqueeze(1), 0, stage[:, 3:4]), (v.dst_s.unsqueeze(1), 1, stage[:, 2:3]),
                                (v.ew_s.unsqueeze(1), 0, stagef[:, :]), (v.ea_s, 0, stager[:, :]))):
                            pool.indirect_dma_start(to, bass.IndirectOffsetOnAxis(ap=stage[:, at:at + 1], axis=0), val, None
                                                    ).then_inc(s_put[n], 16)
                        for n in range(4):
                            pool.wait_ge(s_put[n], 16 * t + 16)
                    pool.sem_inc(s_all, 1)
                with pool.Else():
                    pool.wait_ge(s_own, 1)
        end_phase()


def unit(s, j):
    return 2 * s.k + j + 1


def uses(s):
    return 16 * s.half + 16


def dense_and_gather(nc, sb0, sem, bank, w, vec, v):
    ph = ExitStack()

    def sb(name, shape, dt=F32):
        return sb0(name, shape, dt, ph)

    with ph:
        xin = [sb(f"xin{h}", [P, 2, CH * C]) for h in range(2)]
        xT = [[sb(f"xT{h}{j}", [P, 512]) for j in range(2)] for h in range(2)]
        y1 = [[sb(f"y1{h}{j}", [P, 512]) for j in range(2)] for h in range(2)]
        a = [[sb(f"a{n}{j}", [P, 512]) for j in range(2)] for n in range(2)]
        b = [[sb(f"b{n}{j}", [P, 512]) for j in range(2)] for n in range(2)]
        sT = [sb(f"sT{j}", [P, 512]) for j in range(2)]
        sqf = [sb(f"sqf{j}", [P, 512]) for j in range(2)]
        yrow = [sb(f"yrow{j}", [P, 512]) for j in range(2)]
        x1row = [sb(f"x1row{j}", [P, 512]) for j in range(2)]
        orow = [sb(f"orow{j}", [P, 512]) for j in range(2)]
        ssum = sb("ssum", [P, 2 * CH])
        logs = sb("logs", [P, 2, 2 * CH])
        scale = sb("scale", [P, 2, 2 * CH])
        xe = [sb(f"xe{h}", [P, 4, 2 * ROW]) for h in range(2)]
        xeT = sb("xeT", [P, 512])
        isrc = [sb(f"isrc{h}", [P, 4], I32) for h in range(2)]
        idst = [sb(f"idst{h}", [P, 4], I32) for h in range(2)]
        p1, p2, pv, pe_, pf = bank[0:2], bank[2:4], bank[4], bank[5], bank[6:8]

        s_xin = [sem(f"s_xin{h}") for h in range(2)]
        s_is = [sem(f"s_is{h}") for h in range(2)]
        s_id = [sem(f"s_id{h}") for h in range(2)]
        s_xe = [sem(f"s_xe{h}") for h in range(2)]
        s_xd = [sem(f"s_xd{h}") for h in range(2)]
        s_yst = [sem(f"s_yst{j}") for j in range(2)]
        s_xst = [sem(f"s_xst{j}") for j in range(2)]
        s_ost = [sem(f"s_ost{j}") for j in range(2)]
        (s_xTp, s_xT, s_h1, s_h2, s_sq1, s_sq2, s_v1, s_v2, s_ln1, s_ln2, s_rs1, s_rs2, s_u1, s_u2, s_e1, s_e2,
         s_g1, s_g2, s_y1, s_y2, s_sT, s_fp, s_fq, s_red, s_ln, s_sc, s_x1, s_o, s_yp, s_yr, s_eTp, s_eT, s_lgp, s_lg,
         s_xwp, s_xw, s_cj) = [sem(n) for n in (
             "s_xTp s_xT s_h1 s_h2 s_sq1 s_sq2 s_v1 s_v2 s_ln1 s_ln2 s_rs1 s_rs2 s_u1 s_u2 s_e1 s_e2 "
             "s_g1 s_g2 s_y1 s_y2 s_sT s_fp s_fq s_red s_ln s_sc s_x1 s_o s_yp s_yr s_eTp s_eT s_lgp s_lg "
             "s_xwp s_xw s_cj").split()]
        sq, var, lns, rs, us, es, gs, ys = (s_sq1, s_sq2), (s_v1, s_v2), (s_ln1, s_ln2), (s_rs1, s_rs2), (
            s_u1, s_u2), (s_e1, s_e2), (s_g1, s_g2), (s_y1, s_y2)
        ph_ = (p1, p2)
        hs = (s_h1, s_h2)
        x_units = v.x.rearrange("(d p c) w -> d p (c w)", p=P, c=CH)

        def by_node(table):
            return table.rearrange("(d p c) f -> d p (c f)", p=P, c=CH)

        with nc.Block() as block:
            @block.sync
            def _(sp):
                def load(s):
                    if s.runs():
                        after_apart(sp, s_xTp, unit(s.back(2), 1), v.s_passed)
                        sp.dma_start(xin[s.odd][:, :, :], x_units[bass.ds(2 * s.k, 2)].rearrange("j p n -> p j n")
                                     ).then_inc(s_xin[s.odd], 16)
                        after_apart(sp, s_xe[s.odd], 128 * s.half, v.s_passed)
                        sp.dma_start(isrc[s.odd][:, :], v.srci[:, bass.ds(4 * s.k, 4)]).then_inc(s_is[s.odd], 16)
                        sp.dma_start(idst[s.odd][:, :], v.dsti[:, bass.ds(4 * s.k, 4)]).then_inc(s_id[s.odd], 16)

                def body(s):
                    load(s.back(-1))
                    e = s.back(1)
                    if e.runs():
                        after_apart(sp, s_xe[e.odd], 128 * e.half + 128, v.s_passed)
                        for h in range(2):
                            sp.dma_start(v.xd_d[:, bass.ds(4 * e.k, 4), :].rearrange("p (c h) f -> p h c f", h=2)[:, h],
                                         xe[e.odd][:, 2 * h:2 * h + 2, ROW:ROW + C]).then_inc(s_xd[e.odd], 16)
                        for j in range(2):
                            after_apart(sp, s_yr, unit(e, j), v.s_passed)
                            sp.dma_start(by_node(v.y_table)[2 * e.k + j], yrow[j][:, :]).then_inc(s_yst[j], 16)
                    f = s.back(2)
                    if f.runs():
                        for j in range(2):
                            after_apart(sp, s_x1, unit(f, j), v.s_passed)
                            sp.dma_start(by_node(v.x1_table)[2 * f.k + j], x1row[j][:, :]).then_inc(s_xst[j], 16)
                            after_apart(sp, s_o, unit(f, j), v.s_passed)
                            sp.dma_start(by_node(v.out)[2 * f.k + j], orow[j][:, :]).then_inc(s_ost[j], 16)
                load(Step(0, 0, 0))
                run_steps(sp, body)
                for j in range(2):
                    sp.wait_ge(s_yst[j], 16 * STEPS)
                    sp.wait_ge(s_xst[j], 16 * STEPS)
                    sp.wait_ge(s_ost[j], 16 * STEPS)
                sp.wait_ge(s_xd[0], 32 * (STEPS // 2 + 1))
                sp.wait_ge(s_xd[1], 32 * (STEPS // 2))

            @block.gpsimd
            def _(pool):
                def body(s):
                    if not s.runs():
                        return
                    after_apart(pool, s_is[s.odd], uses(s), v.s_passed)
                    after_apart(pool, s_id[s.odd], uses(s), v.s_passed)
                    after_apart(pool, s_eTp, s.k - 1, v.s_passed)
                    after_apart(pool, s_cj, s.k - 1, v.s_passed)
                    after_apart(pool, s_xd[s.odd], 32 * s.half, v.s_passed)
                    for t in range(4):
                        for n, (i, rows) in enumerate(((isrc, v.xs), (idst, v.xt))):
                            pool.indirect_dma_start(xe[s.odd][:, t, n * ROW:(n + 1) * ROW], None, rows,
                                                    bass.IndirectOffsetOnAxis(ap=i[s.odd][:, t:t + 1], axis=0)
                                                    ).then_inc(s_xe[s.odd], 16)
                run_steps(pool, body)

            @block.tensor
            def _(pe):
                def x_turn(s, j):
                    if j == 0:
                        after(pe, s_xin[s.odd], uses(s))
                    after(pe, s_u1, unit(s.back(1), j))
                    for m in range(4):
                        z = nc.tensor.transpose(
                            p1[j][:, m * P:(m + 1) * P],
                            xin[s.odd][:, j, m * P:(m + 1) * P], v.ident)
                    z.then_inc(s_xTp, 1)

                def layer(n, s, j):
                    src = (xT, y1)[n][s.odd][j]
                    after(pe, (s_xT, s_y1)[n], unit(s, j))
                    if n:
                        after(pe, s_u2, unit(s.back(1), j))
                    nc.tensor.matmul(ph_[n][j][:, :], (v.w1c, v.w2c)[n][:, :], src[:, :], start=True, stop=True
                                     ).then_inc(hs[n], 1)

                def variance(n, s, j):
                    after(pe, sq[n], unit(s, j))
                    if n == 1 and j == 0:
                        after(pe, s_ln1, unit(s, 1))
                    elif n == 1:
                        after(pe, s_ln2, unit(s, 0))
                    elif j == 0:
                        after(pe, s_ln2, unit(s.back(1), 1))
                    else:
                        after(pe, s_ln1, unit(s, 0))
                    nc.tensor.matmul(pv[:, :], w("jbd"), a[n][j][:, :], start=True, stop=True).then_inc(var[n], 1)

                def y_turn(s, j):
                    after(pe, s_yr, unit(s, 0)) if j else after(pe, s_xw, s.k + 1)
                    after(pe, s_y1, unit(s, j))
                    for m in range(4):
                        z = nc.tensor.transpose(pe_[:, m * P:(m + 1) * P], y1[s.odd][j][:, m * P:(m + 1) * P], v.ident)
                    z.then_inc(s_yp, 1)

                def final(s, j):
                    after(pe, s_sT, unit(s, j))
                    after(pe, s_o, unit(s.back(1), j))
                    for m in range(4):
                        z = nc.tensor.matmul(pf[j][:, m * P:(m + 1) * P], sT[j][:, m * P:(m + 1) * P], w("cbd"),
                                             start=True, stop=True)
                    z.then_inc(s_fp, 1)

                def edge_turn(s):
                    after(pe, s_xe[s.odd], 128 * s.half + 128)
                    after(pe, s_yr, unit(s.back(1), 1))
                    for t in range(4):
                        z = nc.tensor.transpose(pe_[:, t * P:(t + 1) * P], xe[s.odd][:, t, 1:1 + 2 * C], v.ident)
                    z.then_inc(s_eTp, 1)

                def edge_logits(s):
                    after(pe, s_eT, s.k + 1)
                    for t in range(4):
                        z = nc.tensor.matmul(pe_[:, t * 8:t * 8 + 8], xeT[:, t * P:(t + 1) * P], v.lgw[:, :],
                                             start=True, stop=True)
                    z.then_inc(s_lgp, 1)

                def edge_features(s):
                    after(pe, s_lg, s.k + 1)
                    for t in range(4):
                        z = nc.tensor.matmul(pe_[:, t * P:(t + 1) * P], xeT[:, t * P:(t + 1) * P], w("w1"),
                                             start=True, stop=True)
                    z.then_inc(s_xwp, 1)

                def body(s):
                    e, f = s.back(1), s.back(2)
                    if s.runs():
                        x_turn(s, 0), x_turn(s, 1)
                    if e.runs():
                        layer(1, e, 0), layer(1, e, 1)
                    if f.runs():
                        final(f, 0), final(f, 1)
                    if s.runs():
                        layer(0, s, 0), layer(0, s, 1)
                    if e.runs():
                        y_turn(e, 0), variance(1, e, 0), y_turn(e, 1), variance(1, e, 1)
                    if s.runs():
                        edge_turn(s), variance(0, s, 0), edge_logits(s), variance(0, s, 1), edge_features(s)
                run_steps(pe, body)

            @block.scalar
            def _(act):
                act.preload_act_table_set("natural_log_exp_and_others")
                bias = ((v.b1c, vec(BE1)), (v.b2c_dense, vec(BE2)))
                gain = (vec(G1), vec(G2))

                def x_copy(s, j):
                    after(act, s_xTp, unit(s, j))
                    after(act, s_sT, unit(s.back(2), j))
                    nc.scalar.activation(xT[s.odd][j][:, :], p1[j][:, :], ACT.Copy).then_inc(s_xT, 1)

                def square(n, s, j):
                    after(act, hs[n], unit(s, j))
                    after(act, ys[n], unit(s.back(1), j))
                    nc.scalar.activation(a[n][j][:, :], ph_[n][j][:, :], ACT.Square, bias=bias[n][0]).then_inc(sq[n], 1)

                def rstd(n, s, j):
                    after(act, var[n], unit(s, j))
                    after(act, (s_y1, s_sT)[n], unit(s.back(1), j))
                    nc.scalar.activation(b[n][j][:, :], pv[:, :], ACT.Ln, bias=vec(EPS)).then_inc(lns[n], 1)
                    after(act, lns[n], unit(s, j))
                    nc.scalar.activation(b[n][j][:, :], b[n][j][:, :], ACT.Exp, scale=-0.5).then_inc(rs[n], 1)

                def elu_exp(n, s, j):
                    after(act, us[n], unit(s, j))
                    nc.scalar.activation(a[n][j][:, :], b[n][j][:, :], ACT.Exp, bias=bias[n][1], scale=gain[n]
                                         ).then_inc(es[n], 1)

                def square_final(s, j):
                    after(act, s_fp, unit(s, j))
                    after(act, s_red, unit(s.back(1), j))
                    nc.scalar.activation(sqf[j][:, :], pf[j][:, :], ACT.Square).then_inc(s_fq, 1)

                def scales(s):
                    after(act, s_red, unit(s, 1))
                    after(act, s_sc, s.back(1).k + 1)
                    nc.scalar.activation(logs[:, 0, :], ssum[:, :], ACT.Ln, bias=vec(EPS), scale=1.0 / C)
                    nc.scalar.activation(logs[:, 1, :], ssum[:, :], ACT.Ln, bias=vec(EPS2), scale=(1.0 + LN_EPS) / C
                                         ).then_inc(s_ln, 1)
                    after(act, s_ln, s.k + 1)
                    after(act, s_o, unit(s.back(1), 1))
                    nc.scalar.activation(scale[:, :, :], logs[:, :, :], ACT.Exp, scale=-0.5).then_inc(s_sc, 1)

                def edge_copy(s):
                    after(act, s_eTp, s.k + 1)
                    after(act, s_xwp, s.k)
                    nc.scalar.activation(xeT[:, :], pe_[:, :], ACT.Copy).then_inc(s_eT, 1)
                    nc.scalar.activation(v.cjp[:, bass.ds(4 * s.k, 4)], xe[s.odd][:, :, 0], ACT.Copy)
                    nc.scalar.activation(v.cip[:, bass.ds(4 * s.k, 4)], xe[s.odd][:, :, 2 * ROW - 1], ACT.Copy).then_inc(s_cj, 1)

                def body(s):
                    e, f = s.back(1), s.back(2)
                    if s.runs():
                        x_copy(s, 0), x_copy(s, 1)
                    if e.runs():
                        square(1, e, 0), square(1, e, 1)
                    if f.runs():
                        square_final(f, 0), square_final(f, 1)
                    if s.runs():
                        square(0, s, 0), square(0, s, 1)
                    if e.runs():
                        rstd(1, e, 0), rstd(1, e, 1)
                    if f.runs():
                        scales(f)
                    if s.runs():
                        edge_copy(s)
                    if e.runs():
                        elu_exp(1, e, 0)
                    if s.runs():
                        rstd(0, s, 0)
                    if e.runs():
                        elu_exp(1, e, 1)
                    if s.runs():
                        rstd(0, s, 1), elu_exp(0, s, 0), elu_exp(0, s, 1)
                run_steps(act, body)

            @block.vector
            def _(dve):
                shift = (v.b1c, v.b2c_dense)
                gain = ((vec(G1), v.be1p), (vec(G2), v.be2p))

                def norm(n, s, j):
                    after(dve, rs[n], unit(s, j))
                    nc.vector.scalar_tensor_tensor(out=b[n][j][:, :], in0=ph_[n][j][:, :], scalar=shift[n], in1=b[n][j][:, :],
                                                   op0=ALU.add, op1=ALU.mult).then_inc(us[n], 1)

                def elu(n, s, j):
                    after(dve, es[n], unit(s, j))
                    nc.vector.tensor_scalar(b[n][j][:, :], b[n][j][:, :], gain[n][0], gain[n][1], ALU.mult, ALU.add
                                            ).then_inc(gs[n], 1)
                    after(dve, gs[n], unit(s, j))
                    if n == 0:
                        after(dve, s_h2, unit(s.back(2), j))
                        after(dve, s_yp, unit(s.back(2), j))
                    to = y1[s.odd][j] if n == 0 else b[1][j]
                    nc.vector.scalar_tensor_tensor(out=to[:, :], in0=a[n][j][:, :], scalar=1.0, in1=b[n][j][:, :],
                                                   op0=ALU.min, op1=ALU.max).then_inc(ys[n], 1)

                def residual(s, j):
                    after(dve, s_y2, unit(s, j))
                    after(dve, s_fp, unit(s.back(1), j))
                    nc.vector.tensor_tensor(sT[j][:, :], b[1][j][:, :], xT[s.odd][j][:, :], ALU.add).then_inc(s_sT, 1)

                def y_rows(s, j):
                    after(dve, s_yp, unit(s, j))
                    after(dve, s_yst[j], 16 * s.k)
                    nc.vector.tensor_scalar(yrow[j][:, :], pe_[:, :], -1.0, None, ALU.add).then_inc(s_yr, 1)

                def reduce(s, j):
                    after(dve, s_fq, unit(s, j))
                    after(dve, s_ln, s.back(1).k + 1)
                    nc.vector.tensor_reduce(ssum[:, j * CH:(j + 1) * CH], sqf[j][:, :].rearrange("p (c f) -> p c f", f=C),
                                            AX.X, ALU.add).then_inc(s_red, 1)

                def rows(s, j, i, to, stored, done):
                    after(dve, s_sc, s.k + 1)
                    after(dve, stored[j], 16 * s.k)
                    nc.vector.tensor_tensor(
                        to[j][:, :].rearrange("p (c f) -> p c f", f=C), pf[j][:, :].rearrange("p (c f) -> p c f", f=C),
                        scale[:, i, j * CH:(j + 1) * CH].unsqueeze(2).to_broadcast([P, CH, C]), ALU.mult).then_inc(done, 1)

                def body(s):
                    e, f = s.back(1), s.back(2)
                    if e.runs():
                        y_rows(e, 0), norm(1, e, 0), y_rows(e, 1), norm(1, e, 1)
                    if f.runs():
                        reduce(f, 0), reduce(f, 1)
                    if s.runs():
                        norm(0, s, 0)
                    if f.runs():
                        rows(f, 0, 0, x1row, s_xst, s_x1), rows(f, 0, 1, orow, s_ost, s_o)
                    if e.runs():
                        elu(1, e, 0), residual(e, 0)
                    if s.runs():
                        after(dve, s_lgp, s.k + 1)
                        nc.vector.tensor_copy(v.lg[:, bass.ds(4 * s.k, 4), :],
                                              pe_[:, 0:32].rearrange("p (t n) -> p t n", n=8)).then_inc(s_lg, 1)
                        norm(0, s, 1)
                    if e.runs():
                        elu(1, e, 1), residual(e, 1)
                    if f.runs():
                        rows(f, 1, 0, x1row, s_xst, s_x1), rows(f, 1, 1, orow, s_ost, s_o)
                    if s.runs():
                        after(dve, s_xwp, s.k + 1)
                        nc.vector.tensor_copy(v.xw[:, bass.ds(4 * s.k, 4), :],
                                              pe_[:, :].rearrange("p (t n) -> p t n", n=2 * C)).then_inc(s_xw, 1)
                        elu(0, s, 0), elu(0, s, 1)
                run_steps(dve, body)


class Rows:

    def __init__(self, nc, v, bank, sb, s_chain, s_rows, s_turned):
        self.nc, self.v, self.bank = nc, v, bank
        self.s_chain, self.s_rows, self.s_turned = s_chain, s_rows, s_turned
        self.links = self.rounds = 0
        self.turns = 0
        self.carry = sb("carry", [HEADS, 2, RQ + 1])

    def link(self, ins):
        self.links += 1
        ins.then_inc(self.s_chain, 1)
        self.nc.vector.wait_ge(self.s_chain, self.links)

    def turned(self, ins):
        self.rounds += 1
        ins.then_inc(self.s_rows, 1)
        self.nc.vector.wait_ge(self.s_turned, self.rounds)

    def _carry(self, heads, mask, op0, op1, first, backward):
        nc, c = self.nc, self.carry[0:heads, 0, :]
        turned = self.bank[6][0:heads, 0:RQ]
        m = self.v.tmask[0:heads, mask, :]
        if backward:
            self.link(nc.vector.memset(c[:, RQ:RQ + 1], first))
            ins = nc.vector.tensor_tensor_scan(c[:, 0:RQ][:, ::-1], m[:, ::-1], turned[:, ::-1], first, op0, op1)
        else:
            self.link(nc.vector.memset(c[:, 0:1], first))
            ins = nc.vector.tensor_tensor_scan(c[:, 1:RQ + 1], m, turned, first, op0, op1)
        self.turned(ins)

    def forward(self, x, heads, largest):
        nc, v = self.nc, self.v
        inner, outer, mask, op0, op1, first = (
            (v.fresh, v.prefresh, 1, ALU.add, ALU.max, -BIG) if largest else (v.same, v.pre, 0, ALU.mult, ALU.add, 0.0))
        for h in range(heads):
            ins = nc.vector.tensor_tensor_scan(x[:, h, :], inner[:, :], x[:, h, :], first, op0, op1)
        self.turned(ins)
        self._carry(heads, mask, op0, op1, first, False)
        for h in range(heads):
            ins = nc.vector.scalar_tensor_tensor(out=x[:, h, :], in0=outer[:, :], scalar=self.bank[7][0:RQ, h:h + 1],
                                                 in1=x[:, h, :], op0=op0, op1=op1)
        self.link(ins)

    def spread(self, x, heads):
        nc, v = self.nc, self.v
        for h in range(heads):
            ins = nc.vector.tensor_tensor(x[:, h, :], x[:, h, :], v.last[:, :], ALU.mult)
        self.link(ins)
        for h in range(heads):
            ins = nc.vector.tensor_tensor_scan(x[:, h, ::-1], v.more[:, ::-1], x[:, h, ::-1], 0.0, ALU.mult, ALU.add)
        self.turned(ins)
        self._carry(heads, 2, ALU.mult, ALU.add, 0.0, True)
        for h in range(heads):
            ins = nc.vector.scalar_tensor_tensor(out=x[:, h, :], in0=v.suf[:, :], scalar=self.bank[7][0:RQ, h:h + 1],
                                                 in1=x[:, h, :], op0=ALU.mult, op1=ALU.add)
        self.link(ins)

    def turn(self, x, heads, backward):
        nc, v, c = self.nc, self.v, self.carry
        end = 0 if backward else 255
        self.turns += 1
        nc.tensor.wait_ge(self.s_rows, self.turns)
        nc.tensor.transpose(self.bank[6][0:heads, 0:RQ], x[:, 0:heads, end], v.ident[0:RQ, 0:RQ]).then_inc(self.s_turned, 1)
        self.turns += 1
        nc.tensor.wait_ge(self.s_rows, self.turns)
        at = 1 if backward else 0
        nc.tensor.transpose(self.bank[7][0:RQ, 0:heads], c[0:heads, 0, at:at + RQ], v.ident[0:heads, 0:heads]
                            ).then_inc(self.s_turned, 1)


def softmax(nc, sb0, sem, bank, v, layer):
    H = HEADS if layer == 1 else 1
    ph = ExitStack()

    def sb(name, shape, dt=F32):
        return sb0(f"{name}{layer}", shape, dt, ph)

    with ph:
        z = sb("z", [RQ, 2 * H, 256])
        top = sb("top", [RQ, H, 256])
        den = sb("den", [RQ, H, 256])
        s_turn, s_raw, s_chain, s_rows, s_turned, s_d, s_exp, s_w, s_back, s_out = [sem(n) for n in (
            "s_turn s_raw s_chain s_rows s_turned s_d s_exp s_w s_back s_out").split()]
        rows = Rows(nc, v, bank, sb, s_chain, s_rows, s_turned)
        sources = 2 * H if layer == 1 else 1
        first = 0 if layer == 1 else 2

        def half(n, s):
            return bank[n // 2][0:RQ, (n % 2) * 256 + s * P:(n % 2) * 256 + (s + 1) * P]

        def slot(n, s):
            return bank[n // 2][:, (n % 2) * 256 + s * P:(n % 2) * 256 + s * P + RQ]

        with nc.Block() as block:
            @block.tensor
            def _(pe):
                for n in range(sources):
                    for s in range(2):
                        t = nc.tensor.transpose(half(n, s), v.lg[:, s::2, first + n], v.ident)
                t.then_inc(s_turn, 1)
                rows.turn(top, H, False)
                rows.turn(top, H, True)
                rows.turn(den, H, False)
                rows.turn(den, H, True)
                pe.wait_ge(s_w, 1)
                for n in range(2 * H):
                    for s in range(2):
                        t = nc.tensor.transpose(slot(n, s), z[:, n, s * P:(s + 1) * P], v.ident[0:RQ, 0:RQ])
                t.then_inc(s_back, 1)

            @block.scalar
            def _(act):
                act.preload_act_table_set("natural_log_exp_and_others")
                act.wait_ge(s_turn, 1)
                for b in range(-(-sources // 2)):
                    k = min(2, sources - 2 * b)
                    t = nc.scalar.activation(z[:, 2 * b:2 * b + k, :], bank[b][0:RQ, 0:256 * k].rearrange(
                        "p (n j) -> p n j", j=256), ACT.Copy)
                t.then_inc(s_raw, 1)
                act.wait_ge(s_d, 1)
                nc.scalar.activation(z[:, :, :], z[:, :, :], ACT.Exp).then_inc(s_exp, 1)

            @block.vector
            def _(dve):
                link = rows.link
                dve.wait_ge(s_raw, 1)
                if layer == 2:
                    link(nc.vector.tensor_tensor(z[:, 0, :], z[:, 0, :], v.adc[:, 0, :], ALU.add))
                    link(nc.vector.tensor_copy(z[:, 1, :], v.adc[:, 1, :]))
                k = 2 * H if layer == 1 else 1
                link(nc.vector.scalar_tensor_tensor(out=z[:, 0:k, :], in0=z[:, 0:k, :], scalar=SLOPE, in1=z[:, 0:k, :],
                                                    op0=ALU.mult, op1=ALU.max))
                link(nc.vector.tensor_copy(top[:, :, :], z[:, 0:H, :]))
                rows.forward(top, H, True)
                rows.spread(top, H)
                link(nc.vector.tensor_tensor(top[:, :, :], top[:, :, :], z[:, H:2 * H, :], ALU.max))
                nc.vector.tensor_tensor(z[:, 0:H, :], z[:, 0:H, :], top[:, :, :], ALU.subtract)
                nc.vector.tensor_tensor(z[:, H:2 * H, :], z[:, H:2 * H, :], top[:, :, :], ALU.subtract).then_inc(s_d, 1)
                dve.wait_ge(s_exp, 1)
                link(nc.vector.tensor_copy(den[:, :, :], z[:, 0:H, :]))
                rows.forward(den, H, False)
                rows.spread(den, H)
                link(nc.vector.scalar_tensor_tensor(out=den[:, :, :], in0=den[:, :, :], scalar=SM_EPS, in1=z[:, H:2 * H, :],
                                                    op0=ALU.add, op1=ALU.add))
                link(nc.vector.reciprocal(den[:, :, :], den[:, :, :]))
                nc.vector.tensor_tensor(z[:, 0:H, :], z[:, 0:H, :], den[:, :, :], ALU.mult)
                link(nc.vector.tensor_tensor(z[:, H:2 * H, :], z[:, H:2 * H, :], den[:, :, :], ALU.mult))
                for h in range(H, 2 * H):
                    t = nc.vector.tensor_tensor(z[:, h, :], z[:, h, :], v.last[:, :], ALU.mult)
                t.then_inc(s_w, 1)
                dve.wait_ge(s_back, 1)
                for n in range(2 * H):
                    t = nc.vector.tensor_copy(
                        v.att[:, :, n].rearrange("p (q s) -> p s q", s=2),
                        bank[n // 2][:, (n % 2) * 256:(n % 2) * 256 + 256].rearrange("p (s q) -> p s q", s=2)[:, :, 0:RQ])
                t.then_inc(s_out, 1)
                dve.wait_ge(s_out, 1)


def aggregate1(nc, sb0, sem, bank, w, vec, v):
    ph = ExitStack()

    def sb(name, shape, dt=F32):
        return sb0(name + "_a1", shape, dt, ph)

    with ph:
        both = [sb(f"both{h}", [P, 4, 2, C]) for h in range(2)]
        msg = [sb(f"msg{h}", [P, 4, C]) for h in range(2)]
        keep = [sb(f"keep{h}", [C, 512]) for h in range(2)]
        run = [sb(f"run{h}", [C, 512]) for h in range(2)]
        a = [sb(f"a{h}", [P, 256]) for h in range(2)]
        b = [sb(f"b{h}", [P, 256]) for h in range(2)]
        yT = [sb(f"yT{h}", [P, 256]) for h in range(2)]
        yrow = [sb(f"yrow{h}", [P, 4, C]) for h in range(2)]
        ilast = [sb(f"ilast{h}", [P, 4], I32) for h in range(2)]
        s_keep, s_il, s_sc = ([sem(f"{n}{h}") for h in range(2)] for n in ("s_keep", "s_il", "s_sc"))
        (s_both, s_msg, s_fp, s_run, s_h, s_sq, s_var, s_ln, s_rs, s_u, s_e, s_g, s_y, s_yT, s_yp, s_yr, s_xp, s_xc
         ) = [sem(n) for n in "s_both s_msg s_fp s_run s_h s_sq s_var s_ln s_rs s_u s_e s_g s_y s_yT s_yp s_yr s_xp s_xc".split()]

        with nc.Block() as block:
            @block.sync
            def _(sp):
                def load(s):
                    if s.runs():
                        after_apart(sp, s_run, s.k - 1, v.s_passed)
                        sp.dma_start(keep[s.odd][:, :], v.same_d[bass.ds(512 * s.k, 512)].unsqueeze(0).to_broadcast([C, 512])
                                     ).then_inc(s_keep[s.odd], 16)
                        after_apart(sp, s_sc[s.odd], 64 * s.half, v.s_passed)
                        sp.dma_start(ilast[s.odd][:, :], v.lasti[:, bass.ds(4 * s.k, 4)]).then_inc(s_il[s.odd], 16)
                load(Step(0, 0, 0))
                run_steps(sp, lambda s: load(s.back(-1)))

            @block.gpsimd
            def _(pool):
                def body(s):
                    f = s.back(2)
                    if f.runs():
                        after_apart(pool, s_il[f.odd], uses(f), v.s_passed)
                        after_apart(pool, s_yr, f.k + 1, v.s_passed)
                        for t in range(4):
                            pool.indirect_dma_start(v.y_table, bass.IndirectOffsetOnAxis(ap=ilast[f.odd][:, t:t + 1], axis=0),
                                                    yrow[f.odd][:, t, :], None, bounds_check=NP - 1, oob_is_err=False
                                                    ).then_inc(s_sc[f.odd], 16)
                run_steps(pool, body)
                pool.wait_ge(s_sc[0], 64 * (STEPS // 2 + 1))
                pool.wait_ge(s_sc[1], 64 * (STEPS // 2))

            @block.tensor
            def _(pe):
                def body(s):
                    e, f = s.back(1), s.back(2)
                    if f.runs():
                        after(pe, s_yT, f.k + 1)
                        after(pe, s_yr, f.k)
                        for c in range(2):
                            t = nc.tensor.transpose(bank[5][:, c * P:(c + 1) * P], yT[f.odd][:, c * P:(c + 1) * P], v.ident)
                        t.then_inc(s_yp, 1)
                        after(pe, s_xc, f.k)
                        for c in range(2):
                            t = nc.tensor.matmul(bank[6][:, c * 132:(c + 1) * 132], yT[f.odd][:, c * P:(c + 1) * P],
                                                 v.r2[:, :], start=True, stop=True)
                        t.then_inc(s_xp, 1)
                    if s.runs():
                        after(pe, s_msg, s.k + 1)
                        after_apart(pe, s_run, s.k - 1, v.s_passed)
                        for t in range(4):
                            z = nc.tensor.transpose(bank[s.odd][0:C, t * P:(t + 1) * P], msg[s.odd][:, t, :], v.ident)
                        z.then_inc(s_fp, 1)
                    if e.runs():
                        after(pe, s_sq, e.k + 1)
                        after(pe, s_ln, e.k)
                        nc.tensor.matmul(bank[4][:, 0:256], w("jbd"), a[e.odd][:, :], start=True, stop=True).then_inc(s_var, 1)
                    if s.runs():
                        centre_halves(nc, pe, s, bank, w, run, s_run, s_u, s_h)
                run_steps(pe, body)

            @block.scalar
            def _(act):
                act.preload_act_table_set("natural_log_exp_and_others")

                def body(s):
                    e, f = s.back(1), s.back(2)
                    if e.runs():
                        norm_scale(nc, act, e, bank, a, b, v.b1c, vec(EPS), s_h, s_y, s_sq, s_var, s_ln, s_rs)
                    if f.runs():
                        after(act, s_yp, f.k + 1)
                        after(act, s_sc[f.odd], 64 * f.half)
                        for c in range(2):
                            z = nc.scalar.activation(yrow[f.odd][:, c::2, :], bank[5][:, c * P:(c + 1) * P].rearrange(
                                "p (h f) -> p h f", h=2), ACT.Copy)
                        z.then_inc(s_yr, 1)
                    if e.runs():
                        after(act, s_u, e.k + 1)
                        nc.scalar.activation(a[e.odd][:, :], b[e.odd][:, :], ACT.Exp, bias=vec(BE1), scale=vec(G1)).then_inc(s_e, 1)
                    if f.runs():
                        after(act, s_xp, f.k + 1)
                        tiles = v.xw[:, bass.ds(4 * f.k, 4), :]
                        logit = v.lg[:, bass.ds(4 * f.k, 4), :]
                        for c in range(2):
                            from_ = bank[6][:, c * 132:(c + 1) * 132].rearrange("p (h n) -> p h n", h=2)
                            nc.scalar.activation(tiles[:, c::2, C:2 * C], from_[:, :, 0:C], ACT.Copy)
                            z = nc.scalar.activation(logit[:, c::2, 0:2], from_[:, :, C:C + 2], ACT.Copy)
                        z.then_inc(s_xc, 1)
                run_steps(act, body)

            @block.vector
            def _(dve):
                def body(s):
                    e = s.back(1)
                    if s.runs():
                        after(dve, s_msg, s.k - 1)
                        nc.vector.tensor_tensor(
                            both[s.odd][:, :, :, :].rearrange("p t n (h c) -> p (t n h) c", h=HEADS),
                            v.xw[:, bass.ds(4 * s.k, 4), :].rearrange("p t (n c) -> p (t n) c", c=C // HEADS),
                            v.att[:, bass.ds(4 * s.k, 4), :].rearrange("p t n -> p (t n)").unsqueeze(2).to_broadcast(
                                [P, 32, C // HEADS]), ALU.mult).then_inc(s_both, 1)
                        after(dve, s_both, s.k + 1)
                        after(dve, s_fp, s.k - 1)
                        nc.vector.tensor_tensor(msg[s.odd][:, :, :], both[s.odd][:, :, 0, :], both[s.odd][:, :, 1, :], ALU.add
                                                ).then_inc(s_msg, 1)
                    if e.runs():
                        norm_apply(nc, dve, e, bank, b, v.b1c, s_rs, s_u)
                    if s.runs():
                        segment_scan(nc, dve, s, bank, keep, run, s_keep, s_fp, s_h, s_run)
                    if e.runs():
                        elu_rows(nc, dve, e, a, b, yT, vec(G1), v.be1p, s_e, s_g, s_y, s_xp)
                        after(dve, s_y, e.k + 1)
                        nc.vector.tensor_scalar(yT[e.odd][:, :], yT[e.odd][:, :], -1.0, None, ALU.add).then_inc(s_yT, 1)
                run_steps(dve, body)


def centre_halves(nc, pe, s, bank, w, run, s_run, s_u, s_h):
    after(pe, s_run, s.k + 1)
    after(pe, s_u, s.k - 1)
    nc.tensor.matmul(bank[2 + s.odd][:, 0:256], w("clo", C), run[s.odd][:, 0:256], start=True, stop=False)
    nc.tensor.matmul(bank[2 + s.odd][:, 0:256], w("chi", C), run[s.odd][:, 256:512], start=False, stop=True).then_inc(s_h, 1)


def segment_scan(nc, dve, s, bank, keep, run, s_keep, s_fp, s_h, s_run):
    after(dve, s_keep[s.odd], uses(s))
    after(dve, s_fp, s.k + 1)
    after(dve, s_h, s.k - 1)
    after(dve, s_run, s.k)
    carry = 0.0 if isinstance(s.k, int) and s.k == 0 else run[1 - s.odd][:, 511:512]
    nc.vector.tensor_tensor_scan(run[s.odd][:, :], keep[s.odd][:, :], bank[s.odd][0:C, :], carry, ALU.mult, ALU.add
                                 ).then_inc(s_run, 1)


def norm_scale(nc, act, s, bank, a, b, shift, eps, s_h, s_y, s_sq, s_var, s_ln, s_rs):
    after(act, s_h, s.k + 1)
    after(act, s_y, s.k - 1)
    nc.scalar.activation(a[s.odd][:, :], bank[2 + s.odd][:, 0:256], ACT.Square, bias=shift).then_inc(s_sq, 1)
    after(act, s_var, s.k + 1)
    nc.scalar.activation(b[s.odd][:, :], bank[4][:, 0:256], ACT.Ln, bias=eps).then_inc(s_ln, 1)
    after(act, s_ln, s.k + 1)
    nc.scalar.activation(b[s.odd][:, :], b[s.odd][:, :], ACT.Exp, scale=-0.5).then_inc(s_rs, 1)


def norm_apply(nc, dve, s, bank, b, shift, s_rs, s_u):
    after(dve, s_rs, s.k + 1)
    nc.vector.scalar_tensor_tensor(out=b[s.odd][:, :], in0=bank[2 + s.odd][:, 0:256], scalar=shift, in1=b[s.odd][:, :],
                                   op0=ALU.add, op1=ALU.mult).then_inc(s_u, 1)


def elu_rows(nc, dve, s, a, b, to, gain, shift, s_e, s_g, s_y, s_read):
    after(dve, s_e, s.k + 1)
    nc.vector.tensor_scalar(b[s.odd][:, :], b[s.odd][:, :], gain, shift, ALU.mult, ALU.add).then_inc(s_g, 1)
    after(dve, s_g, s.k + 1)
    after(dve, s_read, s.k - 1)
    nc.vector.scalar_tensor_tensor(out=to[s.odd][:, :], in0=a[s.odd][:, :], scalar=1.0, in1=b[s.odd][:, :],
                                   op0=ALU.min, op1=ALU.max).then_inc(s_y, 1)


def gather2(nc, sb0, sem, bank, w, vec, v):
    ph = ExitStack()

    def sb(name, shape, dt=F32):
        return sb0(name + "_g2", shape, dt, ph)

    with ph:
        got = [sb(f"got{h}", [P, 4, C]) for h in range(2)]
        gotT = [sb(f"gotT{h}", [P, 256]) for h in range(2)]
        isrc = [sb(f"isrc{h}", [P, 4], I32) for h in range(2)]
        zc = sb("zc", [RQ, 2, 256])
        s_is, s_ga = ([sem(f"{n}{h}") for h in range(2)] for n in ("s_is", "s_ga"))
        s_turn, s_raw, s_chain, s_rows, s_turned, s_tp, s_t, s_xp, s_xc = [sem(n) for n in (
            "s_turn s_raw s_chain s_rows s_turned s_tp s_t s_xp s_xc").split()]
        rows = Rows(nc, v, bank, sb, s_chain, s_rows, s_turned)

        with nc.Block() as block:
            @block.sync
            def _(sp):
                def load(s):
                    if s.runs():
                        after_apart(sp, s_ga[s.odd], 64 * s.half, v.s_passed)
                        sp.dma_start(isrc[s.odd][:, :], v.srci[:, bass.ds(4 * s.k, 4)]).then_inc(s_is[s.odd], 16)
                load(Step(0, 0, 0))
                run_steps(sp, lambda s: load(s.back(-1)))

            @block.gpsimd
            def _(pool):
                def body(s):
                    if s.runs():
                        after_apart(pool, s_is[s.odd], uses(s), v.s_passed)
                        after_apart(pool, s_tp, s.k - 1, v.s_passed)
                        for t in range(4):
                            pool.indirect_dma_start(got[s.odd][:, t, :], None, v.y_table,
                                                    bass.IndirectOffsetOnAxis(ap=isrc[s.odd][:, t:t + 1], axis=0)
                                                    ).then_inc(s_ga[s.odd], 16)
                run_steps(pool, body)

            @block.tensor
            def _(pe):
                for n in range(2):
                    for s in range(2):
                        t = nc.tensor.transpose(bank[5][0:RQ, n * 256 + s * P:n * 256 + (s + 1) * P], v.lg[:, s::2, n], v.ident)
                t.then_inc(s_turn, 1)
                rows.turn(v.adc, 2, True)

                def body(s):
                    e = s.back(1)
                    if s.runs():
                        after(pe, s_ga[s.odd], 64 * s.half + 64)
                        after(pe, s_t, s.k - 1)
                        for c in range(2):
                            t = nc.tensor.transpose(bank[s.odd][:, c * P:(c + 1) * P],
                                                    got[s.odd][:, 2 * c:2 * c + 2, :].rearrange("p t f -> p (t f)"), v.ident)
                        t.then_inc(s_tp, 1)
                    if e.runs():
                        after(pe, s_t, e.k + 1)
                        after(pe, s_xc, e.k - 1)
                        for c in range(2):
                            t = nc.tensor.matmul(bank[2 + e.odd][:, c * 132:(c + 1) * 132], gotT[e.odd][:, c * P:(c + 1) * P],
                                                 v.r2[:, :], start=True, stop=True)
                        t.then_inc(s_xp, 1)
                run_steps(pe, body)

            @block.scalar
            def _(act):
                act.preload_act_table_set("natural_log_exp_and_others")

                def body(s):
                    e = s.back(1)
                    if e.runs():
                        after(act, s_xp, e.k + 1)
                        nc.scalar.activation(v.xw[:, bass.ds(4 * e.k, 4), 0:C], bank[2 + e.odd][:, 0:264].rearrange(
                            "p (t n) -> p t n", n=66)[:, :, 0:C], ACT.Copy)
                        nc.scalar.activation(v.lg[:, bass.ds(4 * e.k, 4), 2], bank[2 + e.odd][:, 0:264].rearrange(
                            "p (t n) -> p t n", n=66)[:, :, C], ACT.Copy).then_inc(s_xc, 1)
                    if s.runs():
                        after(act, s_tp, s.k + 1)
                        after(act, s_xp, s.k - 1)
                        nc.scalar.activation(gotT[s.odd][:, :], bank[s.odd][:, 0:256], ACT.Copy).then_inc(s_t, 1)
                run_steps(act, body)

            @block.vector
            def _(dve):
                link = rows.link
                dve.wait_ge(s_turn, 1)
                link(nc.vector.tensor_copy(zc[:, :, :], bank[5][0:RQ, :].rearrange("p (n j) -> p n j", j=256)))
                link(nc.vector.tensor_copy(v.adc[:, 0, :], zc[:, 1, :]))
                link(nc.vector.tensor_tensor(v.adc[:, 1, :], zc[:, 0, :], zc[:, 1, :], ALU.add))
                link(nc.vector.scalar_tensor_tensor(out=v.adc[:, 1, :], in0=v.adc[:, 1, :], scalar=SLOPE,
                                                    in1=v.adc[:, 1, :], op0=ALU.mult, op1=ALU.max))
                rows.spread(v.adc, 2)


def aggregate2(nc, sb0, sem, bank, w, vec, v):
    ph = ExitStack()

    def sb(name, shape, dt=F32):
        return sb0(name + "_a2", shape, dt, ph)

    with ph:
        both = [sb(f"both{h}", [P, 4, 2, C]) for h in range(2)]
        msg = [sb(f"msg{h}", [P, 4, C]) for h in range(2)]
        keep = [sb(f"keep{h}", [C, 512]) for h in range(2)]
        run = [sb(f"run{h}", [C, 512]) for h in range(2)]
        a = [sb(f"a{h}", [P, 256]) for h in range(2)]
        b = [sb(f"b{h}", [P, 256]) for h in range(2)]
        zT = [sb(f"zT{h}", [P, 256]) for h in range(2)]
        sT = [sb(f"sT{h}", [P, 256]) for h in range(2)]
        xd = [sb(f"xd{h}", [P, 4 * C]) for h in range(2)]
        sqf = sb("sqf", [P, 256])
        ssum = sb("ssum", [P, 4])
        logs = sb("logs", [P, 4])
        scale = sb("scale", [P, 4])
        xrow = [sb(f"xrow{h}", [P, 4, C]) for h in range(2)]
        ilast = [sb(f"ilast{h}", [P, 4], I32) for h in range(2)]
        s_keep, s_il, s_sc, s_xd = ([sem(f"{n}{h}") for h in range(2)] for n in ("s_keep", "s_il", "s_sc", "s_xd"))
        (s_both, s_msg, s_fp, s_run, s_h, s_sq, s_var, s_ln, s_rs, s_u, s_e, s_g, s_y, s_xp, s_sT, s_cp, s_fq, s_red,
         s_lf, s_sf, s_x1) = [sem(n) for n in (
             "s_both s_msg s_fp s_run s_h s_sq s_var s_ln s_rs s_u s_e s_g s_y s_xp s_sT s_cp s_fq s_red "
             "s_lf s_sf s_x1").split()]

        with nc.Block() as block:
            @block.sync
            def _(sp):
                def load(s):
                    if s.runs():
                        after_apart(sp, s_run, s.k - 1, v.s_passed)
                        sp.dma_start(keep[s.odd][:, :], v.same_d[bass.ds(512 * s.k, 512)].unsqueeze(0).to_broadcast([C, 512])
                                     ).then_inc(s_keep[s.odd], 16)
                        after_apart(sp, s_xp, s.k - 1, v.s_passed)
                        sp.dma_start(xd[s.odd][:, :], v.xd_d[:, bass.ds(4 * s.k, 4), :].rearrange("p t f -> p (t f)")
                                     ).then_inc(s_xd[s.odd], 16)
                        after_apart(sp, s_sc[s.odd], 64 * s.half, v.s_passed)
                        sp.dma_start(ilast[s.odd][:, :], v.lasti[:, bass.ds(4 * s.k, 4)]).then_inc(s_il[s.odd], 16)
                load(Step(0, 0, 0))
                run_steps(sp, lambda s: load(s.back(-1)))

            @block.gpsimd
            def _(pool):
                def body(s):
                    f = s.back(2)
                    if f.runs():
                        after_apart(pool, s_il[f.odd], uses(f), v.s_passed)
                        after_apart(pool, s_x1, f.k + 1, v.s_passed)
                        for t in range(4):
                            pool.indirect_dma_start(v.x1_table, bass.IndirectOffsetOnAxis(ap=ilast[f.odd][:, t:t + 1], axis=0),
                                                    xrow[f.odd][:, t, :], None, bounds_check=NP - 1, oob_is_err=False
                                                    ).then_inc(s_sc[f.odd], 16)
                run_steps(pool, body)
                pool.wait_ge(s_sc[0], 64 * (STEPS // 2 + 1))
                pool.wait_ge(s_sc[1], 64 * (STEPS // 2))

            @block.tensor
            def _(pe):
                def body(s):
                    e, f = s.back(1), s.back(2)
                    if f.runs():
                        after(pe, s_sT, f.k + 1)
                        after(pe, s_x1, f.k)
                        for c in range(2):
                            t = nc.tensor.matmul(bank[5][:, c * P:(c + 1) * P], sT[f.odd][:, c * P:(c + 1) * P], w("cbd"),
                                                 start=True, stop=True)
                        t.then_inc(s_cp, 1)
                    if s.runs():
                        after(pe, s_msg, s.k + 1)
                        after_apart(pe, s_run, s.k - 1, v.s_passed)
                        for t in range(4):
                            z = nc.tensor.transpose(bank[s.odd][0:C, t * P:(t + 1) * P], msg[s.odd][:, t, :], v.ident)
                        z.then_inc(s_fp, 1)
                    if e.runs():
                        after(pe, s_xd[e.odd], uses(e))
                        after(pe, s_sT, e.k)
                        for c in range(2):
                            t = nc.tensor.transpose(bank[6][:, c * P:(c + 1) * P], xd[e.odd][:, c * P:(c + 1) * P], v.ident)
                        t.then_inc(s_xp, 1)
                        after(pe, s_sq, e.k + 1)
                        after(pe, s_ln, e.k)
                        nc.tensor.matmul(bank[4][:, 0:256], w("jbd"), a[e.odd][:, :], start=True, stop=True).then_inc(s_var, 1)
                    if s.runs():
                        centre_halves(nc, pe, s, bank, w, run, s_run, s_u, s_h)
                run_steps(pe, body)

            @block.scalar
            def _(act):
                act.preload_act_table_set("natural_log_exp_and_others")

                def body(s):
                    e, f = s.back(1), s.back(2)
                    if e.runs():
                        norm_scale(nc, act, e, bank, a, b, v.b2c, vec(EPS), s_h, s_y, s_sq, s_var, s_ln, s_rs)
                    if f.runs():
                        after(act, s_cp, f.k + 1)
                        after(act, s_red, f.k)
                        nc.scalar.activation(sqf[:, :], bank[5][:, 0:256], ACT.Square).then_inc(s_fq, 1)
                    if e.runs():
                        after(act, s_u, e.k + 1)
                        nc.scalar.activation(a[e.odd][:, :], b[e.odd][:, :], ACT.Exp, bias=vec(BE2), scale=vec(G2)).then_inc(s_e, 1)
                    if f.runs():
                        final_scale(nc, act, f, ssum, logs, scale, vec(EPS), s_red, s_lf, s_sf, s_x1)
                run_steps(act, body)

            @block.vector
            def _(dve):
                def body(s):
                    e, f = s.back(1), s.back(2)
                    if s.runs():
                        after(dve, s_msg, s.k - 1)
                        nc.vector.tensor_tensor(
                            both[s.odd][:, :, :, :].rearrange("p t n c -> p (t n) c"),
                            v.xw[:, bass.ds(4 * s.k, 4), :].rearrange("p t (n c) -> p (t n) c", c=C),
                            v.att[:, bass.ds(4 * s.k, 4), 0:2].unsqueeze(3).to_broadcast([P, 4, 2, C]), ALU.mult
                        ).then_inc(s_both, 1)
                        after(dve, s_both, s.k + 1)
                        after(dve, s_fp, s.k - 1)
                        nc.vector.tensor_tensor(msg[s.odd][:, :, :], both[s.odd][:, :, 0, :], both[s.odd][:, :, 1, :], ALU.add
                                                ).then_inc(s_msg, 1)
                    if e.runs():
                        norm_apply(nc, dve, e, bank, b, v.b2c, s_rs, s_u)
                    if f.runs():
                        after(dve, s_fq, f.k + 1)
                        after(dve, s_lf, f.k)
                        nc.vector.tensor_reduce(ssum[:, :], sqf[:, :].rearrange("p (t f) -> p t f", f=C), AX.X, ALU.add
                                                ).then_inc(s_red, 1)
                    if s.runs():
                        segment_scan(nc, dve, s, bank, keep, run, s_keep, s_fp, s_h, s_run)
                    if e.runs():
                        elu_rows(nc, dve, e, a, b, zT, vec(G2), v.be2p, s_e, s_g, s_y, s_sT)
                    if f.runs():
                        after(dve, s_sf, f.k + 1)
                        after(dve, s_sc[f.odd], 64 * f.half)
                        for c in range(2):
                            z = nc.vector.tensor_tensor(
                                xrow[f.odd][:, c::2, :], bank[5][:, c * P:(c + 1) * P].rearrange("p (h f) -> p h f", h=2),
                                scale[:, 2 * c:2 * c + 2].unsqueeze(2).to_broadcast([P, 2, C]), ALU.mult)
                        z.then_inc(s_x1, 1)
                        after(dve, s_x1, f.k + 1)
                        nc.vector.tensor_copy(v.x1r[:, bass.ds(4 * f.k, 4), :], xrow[f.odd][:, :, :])
                    if e.runs():
                        after(dve, s_y, e.k + 1)
                        after(dve, s_xp, e.k + 1)
                        after(dve, s_cp, e.k - 1)
                        nc.vector.tensor_tensor(sT[e.odd][:, :], zT[e.odd][:, :], bank[6][:, 0:256], ALU.add).then_inc(s_sT, 1)
                run_steps(dve, body)


def final_scale(nc, act, s, ssum, logs, scale, eps, s_red, s_lf, s_sf, s_done):
    after(act, s_red, s.k + 1)
    after(act, s_sf, s.k)
    nc.scalar.activation(logs[:, :], ssum[:, :], ACT.Ln, bias=eps, scale=1.0 / C).then_inc(s_lf, 1)
    after(act, s_lf, s.k + 1)
    after(act, s_done, s.k)
    nc.scalar.activation(scale[:, :], logs[:, :], ACT.Exp, scale=-0.5).then_inc(s_sf, 1)


def aggregate3(nc, sb0, sem, bank, w, vec, v, s_reviews):
    ph = ExitStack()

    def sb(name, shape, dt=F32):
        return sb0(name + "_a3", shape, dt, ph)

    with ph:
        rv = [sb(f"rv{h}", [P, 4, C]) for h in range(2)]
        rvT = [sb(f"rvT{h}", [P, 256]) for h in range(2)]
        gate = [sb(f"gate{h}", [P, 4, 2]) for h in range(2)]
        gx = [sb(f"gx{h}", [P, 4, C]) for h in range(2)]
        mx = [sb(f"mx{h}", [P, 4, C]) for h in range(2)]
        mr = [sb(f"mr{h}", [P, 4, C]) for h in range(2)]
        msg = [sb(f"msg{h}", [P, 4, C]) for h in range(2)]
        keep = [sb(f"keep{h}", [C, 512]) for h in range(2)]
        run = [sb(f"run{h}", [C, 512]) for h in range(2)]
        hc = [sb(f"hc{h}", [P, 4, C]) for h in range(2)]
        sqf = sb("sqf", [P, 256])
        ssum = sb("ssum", [P, 4])
        logs = sb("logs", [P, 4])
        scale = sb("scale", [P, 4])
        orow = [sb(f"orow{h}", [P, 4, C]) for h in range(2)]
        isrc = [sb(f"isrc{h}", [P, 4], I32) for h in range(2)]
        ilast = [sb(f"ilast{h}", [P, 4], I32) for h in range(2)]
        s_keep, s_il, s_is, s_ga, s_sc, s_rv = ([sem(f"{n}{h}") for h in range(2)] for n in (
            "s_keep", "s_il", "s_is", "s_ga", "s_sc", "s_rv"))
        (s_rp, s_rT, s_gp, s_ge, s_g1, s_g2, s_g3, s_gate, s_mr, s_mx, s_msg, s_fp, s_run, s_hp, s_hc, s_s, s_fq, s_red,
         s_lf, s_sf, s_o) = [sem(n) for n in (
             "s_rp s_rT s_gp s_ge s_g1 s_g2 s_g3 s_gate s_mr s_mx s_msg s_fp s_run s_hp s_hc s_s s_fq s_red "
             "s_lf s_sf s_o").split()]

        with nc.Block() as block:
            @block.sync
            def _(sp):
                def load(s):
                    if s.runs():
                        after_apart(sp, s_ga[s.odd], 64 * s.half, v.s_passed)
                        sp.dma_start(isrc[s.odd][:, :], v.srci[:, bass.ds(4 * s.k, 4)]).then_inc(s_is[s.odd], 16)
                        after_apart(sp, s_rp, s.k - 1, v.s_passed)
                        sp.dma_start(rv[s.odd][:, :, :], v.ea_s.rearrange("(t p) f -> t p f", p=P)[bass.ds(4 * s.k, 4)
                                     ].rearrange("t p f -> p t f")).then_inc(s_rv[s.odd], 16)
                    e = s.back(1)
                    if e.runs():
                        after_apart(sp, s_run, e.k - 1, v.s_passed)
                        sp.dma_start(keep[e.odd][:, :], v.same_d[bass.ds(512 * e.k, 512)].unsqueeze(0).to_broadcast([C, 512])
                                     ).then_inc(s_keep[e.odd], 16)
                        after_apart(sp, s_sc[e.odd], 64 * e.half, v.s_passed)
                        sp.dma_start(ilast[e.odd][:, :], v.lasti[:, bass.ds(4 * e.k, 4)]).then_inc(s_il[e.odd], 16)
                sp.wait_ge(s_reviews, 16)
                load(Step(0, 0, 0))
                run_steps(sp, lambda s: load(s.back(-1)), LAG + 1)

            @block.gpsimd
            def _(pool):
                def body(s):
                    f = s.back(3)
                    if s.runs():
                        after_apart(pool, s_is[s.odd], uses(s), v.s_passed)
                        after_apart(pool, s_mx, s.k - 1, v.s_passed)
                        for t in range(4):
                            pool.indirect_dma_start(gx[s.odd][:, t, :], None, v.x1_table,
                                                    bass.IndirectOffsetOnAxis(ap=isrc[s.odd][:, t:t + 1], axis=0)
                                                    ).then_inc(s_ga[s.odd], 16)
                    if f.runs():
                        after_apart(pool, s_il[f.odd], uses(f), v.s_passed)
                        after_apart(pool, s_o, f.k + 1, v.s_passed)
                        for t in range(4):
                            pool.indirect_dma_start(v.out, bass.IndirectOffsetOnAxis(ap=ilast[f.odd][:, t:t + 1], axis=0),
                                                    orow[f.odd][:, t, :], None, bounds_check=NP - 1, oob_is_err=False
                                                    ).then_inc(s_sc[f.odd], 16)
                run_steps(pool, body, LAG + 1)
                pool.wait_ge(s_sc[0], 64 * (STEPS // 2 + 1))
                pool.wait_ge(s_sc[1], 64 * (STEPS // 2))

            @block.tensor
            def _(pe):
                def body(s):
                    e, f = s.back(1), s.back(2)
                    if s.runs():
                        after(pe, s_rv[s.odd], uses(s))
                        after(pe, s_rT, s.k)
                        for c in range(2):
                            t = nc.tensor.transpose(bank[6][:, c * P:(c + 1) * P],
                                                    rv[s.odd][:, 2 * c:2 * c + 2, :].rearrange("p t f -> p (t f)"), v.ident)
                        t.then_inc(s_rp, 1)
                    if f.runs():
                        after(pe, s_run, f.k + 1)
                        after(pe, s_hc, f.k)
                        for t in range(4):
                            z = nc.tensor.matmul(bank[5][:, t * C:(t + 1) * C], run[f.odd][:, t * P:(t + 1) * P],
                                                 w("cbd", C)[:, 0:C], start=True, stop=True)
                        z.then_inc(s_hp, 1)
                    if e.runs():
                        after(pe, s_msg, e.k + 1)
                        after_apart(pe, s_run, e.k - 1, v.s_passed)
                        for t in range(4):
                            z = nc.tensor.transpose(bank[e.odd][0:C, t * P:(t + 1) * P], msg[e.odd][:, t, :], v.ident)
                        z.then_inc(s_fp, 1)
                    if s.runs():
                        after(pe, s_rT, s.k + 1)
                        after(pe, s_mr, s.k - 1)
                        for c in range(2):
                            t = nc.tensor.matmul(bank[2 + s.odd][:, c * 132:(c + 1) * 132], rvT[s.odd][:, c * P:(c + 1) * P],
                                                 w("rev"), start=True, stop=True)
                        t.then_inc(s_gp, 1)
                run_steps(pe, body, LAG + 1)

            @block.scalar
            def _(act):
                act.preload_act_table_set("natural_log_exp_and_others")

                def body(s):
                    f = s.back(2)
                    if s.runs():
                        after(act, s_rp, s.k + 1)
                        after(act, s_gp, s.k - 1)
                        nc.scalar.activation(rvT[s.odd][:, :], bank[6][:, 0:256], ACT.Copy).then_inc(s_rT, 1)
                    if f.runs():
                        after(act, s_s, f.k + 1)
                        after(act, s_red, f.k)
                        nc.scalar.activation(sqf[:, :], hc[f.odd][:, :, :].rearrange("p t f -> p (t f)"), ACT.Square
                                             ).then_inc(s_fq, 1)
                    if s.runs():
                        after(act, s_gp, s.k + 1)
                        after(act, s_mr, s.k - 1)
                        nc.scalar.activation(gate[s.odd][:, :, :], bank[2 + s.odd][:, 0:264].rearrange(
                            "p (t n) -> p t n", n=66)[:, :, C:C + 2], ACT.Exp, scale=-1.0).then_inc(s_ge, 1)
                    if f.runs():
                        final_scale(nc, act, f, ssum, logs, scale, vec(EPS), s_red, s_lf, s_sf, s_o)
                run_steps(act, body, LAG + 1)

            @block.vector
            def _(dve):
                def body(s):
                    e, f = s.back(1), s.back(2)
                    if f.runs():
                        after(dve, s_hp, f.k + 1)
                        after(dve, s_o, f.k - 1)
                        nc.vector.tensor_tensor(hc[f.odd][:, :, :], bank[5][:, 0:256].rearrange("p (t f) -> p t f", f=C),
                                                v.cip[:, bass.ds(4 * f.k, 4)].unsqueeze(2).to_broadcast([P, 4, C]), ALU.mult
                                                ).then_inc(s_hc, 1)
                    if e.runs():
                        after(dve, s_ga[e.odd], 64 * e.half + 64)
                        after(dve, s_gate, e.k + 1)
                        after(dve, s_msg, e.k - 1)
                        nc.vector.tensor_tensor(mx[e.odd][:, :, :], gx[e.odd][:, :, :],
                                                gate[e.odd][:, :, 0:1].to_broadcast([P, 4, C]), ALU.mult
                                                ).then_inc(s_mx, 1)
                        nc.vector.tensor_tensor(mr[e.odd][:, :, :], bank[2 + e.odd][:, 0:264].rearrange(
                            "p (t n) -> p t n", n=66)[:, :, 0:C], gate[e.odd][:, :, 1:2].to_broadcast([P, 4, C]), ALU.mult
                        ).then_inc(s_mr, 1)
                    if f.runs():
                        after(dve, s_hc, f.k + 1)
                        nc.vector.tensor_tensor(hc[f.odd][:, :, :], hc[f.odd][:, :, :], v.x1r[:, bass.ds(4 * f.k, 4), :], ALU.add
                                                ).then_inc(s_s, 1)
                    if e.runs():
                        after(dve, s_mr, e.k + 1)
                        after(dve, s_fp, e.k - 1)
                        nc.vector.tensor_tensor(msg[e.odd][:, :, :], mx[e.odd][:, :, :], mr[e.odd][:, :, :], ALU.add
                                                ).then_inc(s_msg, 1)
                    if s.runs():
                        g = gate[s.odd]
                        cj = v.cjp[:, bass.ds(4 * s.k, 4)]
                        after(dve, s_ge, s.k + 1)
                        nc.vector.tensor_scalar(g[:, :, :], g[:, :, :], 1.0, None, ALU.add).then_inc(s_g1, 1)
                        after(dve, s_g1, s.k + 1)
                        nc.vector.reciprocal(g[:, :, :], g[:, :, :]).then_inc(s_g2, 1)
                        after(dve, s_g2, s.k + 1)
                        nc.vector.tensor_tensor(g[:, :, 1], g[:, :, 1], v.ewp[:, bass.ds(4 * s.k, 4)], ALU.mult).then_inc(s_g3, 1)
                        after(dve, s_g3, s.k + 1)
                        nc.vector.tensor_tensor(g[:, :, :], g[:, :, :], cj.unsqueeze(2).to_broadcast([P, 4, 2]), ALU.mult
                                                ).then_inc(s_gate, 1)
                    if e.runs():
                        segment_scan(nc, dve, e, bank, keep, run, s_keep, s_fp, s_hp, s_run)
                    if f.runs():
                        after(dve, s_fq, f.k + 1)
                        after(dve, s_lf, f.k)
                        nc.vector.tensor_reduce(ssum[:, :], sqf[:, :].rearrange("p (t f) -> p t f", f=C), AX.X, ALU.add
                                                ).then_inc(s_red, 1)
                        after(dve, s_sf, f.k + 1)
                        after(dve, s_sc[f.odd], 64 * f.half)
                        nc.vector.tensor_tensor(orow[f.odd][:, :, :], hc[f.odd][:, :, :],
                                                scale[:, :].unsqueeze(2).to_broadcast([P, 4, C]), ALU.mult).then_inc(s_o, 1)
                run_steps(dve, body, LAG + 1)


def kernel(x, src, dst, edge_attr_64, edge_weight, node_vec1, node_vec1_n2, L0_gnn_W1, L0_gnn_a1_src, L0_gnn_a1_dst,
           L0_gnn_b1, L0_gnn_W2, L0_gnn_a2_src, L0_gnn_a2_dst, L0_gnn_b2, L0_gnn_ln1_g, L0_gnn_ln1_b, L0_gnn_ln2_g,
           L0_gnn_ln2_b, L1_gnn_prob_w, L1_gnn_review_score_w, L1_gnn_review_w):
    import numpy as np
    import concourse.bacc as bacc
    from concourse.bass_utils import run_bass_kernel_spmd

    f32, i32 = np.float32, np.int32
    xp = np.zeros((NP, C), f32)
    xp[:N] = x
    xs = np.zeros((NP, ROW), f32)
    xs[:N, 0:1] = node_vec1
    xs[:N, 1:ROW] = x
    xt = np.zeros((NP, ROW), f32)
    xt[:N, 0:C] = x
    xt[:N, C:ROW] = node_vec1_n2
    srcp = np.full((EP,), N, i32)
    srcp[:E] = src
    dstp = np.full((EP + 2,), N, i32)
    dstp[0] = -1
    dstp[1:E + 1] = dst
    ewp = np.zeros((EP,), f32)
    ewp[:E] = edge_weight
    eap = np.zeros((EP, C), f32)
    eap[:E] = edge_attr_64

    wts = np.zeros((P, WIDTH), f32)

    def block(name):
        a, b = COLS[name]
        return wts[:, a:b]

    def twice(to, m):
        n = to.shape[1] // 2
        to[0:C, 0:m.shape[1]] = m
        to[C:P, n:n + m.shape[1]] = m

    centre = (np.eye(C) - 1.0 / C).astype(f32)
    block("ident")[:, :] = np.eye(P, dtype=f32)
    twice(block("cbd"), centre)
    twice(block("jbd"), np.full((C, C), 1.0 / C, f32))
    block("clo")[0:C, 0:C] = centre
    block("chi")[0:C, C:P] = centre
    W1, W2 = np.asarray(L0_gnn_W1), np.asarray(L0_gnn_W2)
    twice(block("w1t"), W1.T)
    twice(block("w1"), W1)
    twice(block("w2t"), W2.T)
    twice(block("w2"), W2)
    per = C // HEADS
    for h in range(HEADS):
        rows = slice(h * per, (h + 1) * per)
        low = slice(C + h * per, C + (h + 1) * per)
        block("al1")[rows, h] = L0_gnn_a1_src[h]
        block("al1")[low, h] = L0_gnn_a1_dst[h]
        block("al1")[low, HEADS + h] = L0_gnn_a1_src[h]
        block("al2")[low, HEADS + h] = L0_gnn_a1_dst[h]
    twice(block("sel2"), np.concatenate([np.eye(C, dtype=f32), np.asarray(L0_gnn_a2_src).T, np.asarray(L0_gnn_a2_dst).T], 1))
    twice(block("rev"), np.concatenate([np.asarray(L1_gnn_review_w).T, np.asarray(L1_gnn_prob_w).T,
                                        np.asarray(L1_gnn_review_score_w).T], 1))
    for i, m in ((B1, L0_gnn_b1), (B2, L0_gnn_b2), (G1, L0_gnn_ln1_g), (BE1, L0_gnn_ln1_b), (G2, L0_gnn_ln2_g),
                 (BE2, L0_gnn_ln2_b)):
        block("vec")[0:C, i] = m
        block("vec")[C:P, i] = m
    block("vec")[:, ONE] = 1.0
    block("vec")[:, EPS] = LN_EPS
    block("vec")[:, EPS2] = LN_EPS * LN_EPS

    nc = bacc.Bacc("TRN2", target_bir_lowering=False, num_devices=1)
    arrays = {"x": xp, "xs": xs, "xt": xt, "src": srcp, "dst": dstp, "ew": ewp, "ea": eap, "wts_in": wts}
    args = [nc.dram_tensor(n, a.shape, mybir.dt.from_np(a.dtype), kind="ExternalInput").ap() for n, a in arrays.items()]
    out = nc.dram_tensor("out", (NP, C), F32, kind="ExternalOutput").ap()
    gnn_program(nc, *args, out)
    r = run_bass_kernel_spmd(nc, [arrays], core_ids=[0])
    return r.results[0]["out"][:N]
```

```python
from contextlib import ExitStack

import concourse.bass as bass
from concourse import mybir

ALU = mybir.AluOpType
ACT = mybir.ActivationFunctionType
AX = mybir.AxisListType
F32 = mybir.dt.float32
I32 = mybir.dt.int32

P = 128
C = 64
HEADS = 4
N, E = 100000, 25000
ROW = C + 1
CH = 8
UNIT = P * CH
TILES = -(-E // (4 * P)) * 4
EP = TILES * P
STEPS = TILES // 4
NP = 2 * STEPS * UNIT
assert NP > N and STEPS % 2 == 1
RQ = EP // 256
BIG = 1.0e30
SKIP = 1 << 20
LN_EPS = 1e-5
SM_EPS = 1e-16
SLOPE = 0.2

COLS = {}
WIDTH = 0
for _name, _w in (("ident", P), ("cbd", P), ("jbd", P), ("clo", P), ("chi", P), ("w1t", P), ("w1", P), ("al1", 8),
                  ("al2", 8), ("w2t", P), ("w2", P), ("sel2", 132), ("rev", 132), ("vec", 10)):
    COLS[_name] = (WIDTH, WIDTH + _w)
    WIDTH += _w
B1, B2, G1, BE1, G2, BE2, ONE, EPS, EPS2, ZERO = range(10)


def after(eng, sem, count):
    if isinstance(count, int) and count <= 0:
        return
    eng.wait_ge(sem, count)


def after_apart(eng, sem, count, s_passed):
    after(eng, sem, count)
    if not isinstance(count, int):
        eng.sem_inc(s_passed, 1)


class Step:

    def __init__(self, k, half, odd, quarter=None, rest=None):
        self.k, self.half, self.odd, self.quarter, self.rest = k, half, odd, quarter, rest

    def back(self, n):
        k = self.k - n
        if isinstance(k, int):
            return step(k)
        if self.rest is None:
            return Step(k, self.half + (self.odd - n) // 2, (self.odd - n) % 2)
        return Step(k, self.half + (self.odd - n) // 2, (self.odd - n) % 2,
                    self.quarter + (self.rest - n) // 4, (self.rest - n) % 4)

    def runs(self):
        return not isinstance(self.k, int) or 0 <= self.k < STEPS


def step(k):
    return Step(k, k // 2, k % 2, k // 4, k % 4)


def run_steps(eng, body, lag, ahead=1, unroll=2):
    first = -(-(lag + 2) // unroll)
    end = (STEPS - ahead) // unroll
    for k in range(unroll * first):
        body(step(k))
    with eng.Fori(first, end) as m:
        for i in range(unroll):
            body(Step(2 * m + i, m, i) if unroll == 2 else Step(4 * m + i, 2 * m + i // 2, i % 2, m, i))
    for k in range(unroll * end, STEPS + lag):
        body(step(k))


class Shared:
    pass


def gnn_program(nc, x, xs, xt, src, dst, ew, ea, wts_in, out):
    ctx = ExitStack()

    def sb(name, shape, dt=F32, on=ctx):
        return on.enter_context(nc.sbuf_tensor(name, shape, dt))

    def scratch(name, shape, dt=F32):
        return nc.dram_tensor(name, shape, dt, kind="Internal").ap()

    y_table = scratch("y_table", (NP, C))
    x1_table = scratch("x1_table", (NP, C))
    dst_s = scratch("dst_s", (EP + 2,), I32)
    src_s = scratch("src_s", (EP,), I32)
    ew_s = scratch("ew_s", (EP,))
    ea_s = scratch("ea_s", (EP, C))
    same_d = scratch("same_d", (EP,))
    xd_d = scratch("xd_d", (P, TILES, C))

    with ctx:
        bank = [ctx.enter_context(nc.psum_tensor(f"bank{i}", [P, 512], F32)) for i in range(8)]
        wts = sb("wts", [P, WIDTH])
        w1c = sb("w1c", [P, P])
        w2c = sb("w2c", [P, P])
        r2 = sb("r2", [P, 132])
        lgw = sb("lgw", [P, 8])
        col = sb("col", [P, 6])
        srci = sb("srci", [P, TILES], I32)
        dsti = sb("dsti", [P, TILES], I32)
        lasti = sb("lasti", [P, TILES], I32)
        ewp = sb("ewp", [P, TILES])
        cjp = sb("cjp", [P, TILES])
        cip = sb("cip", [P, TILES])
        lg = sb("lg", [P, TILES, 8])
        att = sb("att", [P, TILES, 8])
        same = sb("same", [RQ, 256])
        fresh = sb("fresh", [RQ, 256])
        more = sb("more", [RQ, 256])
        last = sb("last", [RQ, 256])
        pre = sb("pre", [RQ, 256])
        prefresh = sb("prefresh", [RQ, 256])
        suf = sb("suf", [RQ, 256])
        tmask = sb("tmask", [HEADS, 3, RQ])

        def w(name, rows=P):
            a, b = COLS[name]
            return wts[0:rows, a:b]

        def vec(i):
            return wts[:, COLS["vec"][0] + i:COLS["vec"][0] + i + 1]

        ident = w("ident")
        b1c, b2c, b2c_dense, be1p, be2p = (col[:, i:i + 1] for i in range(5))

        phase_sems = []

        ended = []

        def sem(name):
            s = nc.alloc_semaphore(f"{name}_{len(ended)}")
            phase_sems.append(s)
            return s

        def end_phase():
            nc.clear_and_free_semaphores(list(phase_sems))
            phase_sems.clear()
            ended.append(len(ended))
            nc.all_engine_barrier()

        v = Shared()
        v.x, v.xs, v.xt, v.dst, v.src, v.ew, v.ea, v.wts_in, v.out = x, xs, xt, dst, src, ew, ea, wts_in, out
        v.y_table, v.x1_table, v.dst_s, v.src_s, v.ew_s, v.ea_s, v.same_d, v.xd_d = (
            y_table, x1_table, dst_s, src_s, ew_s, ea_s, same_d, xd_d)
        v.bank, v.wts, v.vec, v.ident, v.w1c, v.w2c, v.r2, v.lgw = bank, wts, vec, ident, w1c, w2c, r2, lgw
        v.b1c, v.b2c, v.b2c_dense, v.be1p, v.be2p = b1c, b2c, b2c_dense, be1p, be2p
        v.srci, v.dsti, v.lasti, v.ewp, v.cjp, v.cip, v.lg, v.att = srci, dsti, lasti, ewp, cjp, cip, lg, att
        v.same, v.fresh, v.more, v.last, v.pre, v.prefresh, v.suf, v.tmask = (
            same, fresh, more, last, pre, prefresh, suf, tmask)
        v.flag = sb("flag", [1, 1], I32)
        v.s_passed = nc.alloc_semaphore("s_passed")
        s_reviews = nc.alloc_semaphore("s_reviews")

        sort_edges(nc, sb, sem, end_phase, v, s_reviews)

        with ExitStack() as ph:
            dc = sb("dc", [RQ, 3, 256], I32, ph)
            df = sb("df", [RQ, 3, 256], F32, ph)
            sc = sb("sc", [RQ, 2, 256], I32, ph)
            turn = sb("turn", [RQ, 4, 256], F32, ph)
            ends = sb("ends", [RQ, 3, HEADS], F32, ph)
            bcol = sb("bcol", [P, 1], F32, ph)
            s_ld = [sem(f"s_ld{i}") for i in range(5)]
            s_v = sem("s_v")
            s_turn = sem("s_turn")
            s_ends = sem("s_ends")
            s_col = sem("s_col")
            s_pt = sem("s_pt")
            s_pe = sem("s_pe")
            s_pw = sem("s_pw")
            s_pb = sem("s_pb")
            s_same = sem("s_same")
            s_st = sem("s_st")
            block = nc.Block()
            with block:
                @block.sync
                def _(sp):
                    for n in range(3):
                        o = (1, 0, 2)[n]
                        sp.dma_start(dc[:, n, :], dst_s[o:o + EP].rearrange("(q j) -> q j", j=256)).then_inc(s_ld[n], 16)
                    sp.dma_start(sc[:, 0, :], src_s.rearrange("(q j) -> q j", j=256)).then_inc(s_ld[3], 16)
                    sp.dma_start(turn[:, 3, :], ew_s.rearrange("(q j) -> q j", j=256)).then_inc(s_ld[4], 16)
                    sp.wait_ge(s_same, 1)
                    sp.dma_start(same_d.rearrange("(q j) -> q j", j=256), same[:, :]).then_inc(s_st, 16)
                    sp.wait_ge(s_st, 16)

                @block.vector
                def _(dve):
                    chain = [0]

                    def link(ins):
                        chain[0] += 1
                        ins.then_inc(s_v, 1)
                        dve.wait_ge(s_v, chain[0])

                    dve.wait_ge(s_pw, 1)
                    nc.vector.tensor_copy(w1c[:, :], bank[3][:, 0:P])
                    nc.vector.tensor_copy(w2c[:, :], bank[3][:, P:2 * P])
                    nc.vector.tensor_copy(r2[:, :], bank[3][:, 2 * P:2 * P + 132])
                    nc.vector.tensor_copy(lgw[:, :], bank[4][:, 0:8])
                    nc.vector.tensor_copy(col[:, 0:2], bank[4][:, 8:10])
                    nc.vector.tensor_tensor(bcol[:, :], vec(B2), bank[4][:, 10:11], ALU.subtract).then_inc(s_col, 1)
                    nc.vector.tensor_scalar(col[:, 3:4], vec(BE1), 1.0, None, ALU.add)
                    nc.vector.tensor_scalar(col[:, 4:5], vec(BE2), 1.0, None, ALU.add)
                    for n in range(3):
                        dve.wait_ge(s_ld[n], 16)
                    link(nc.vector.tensor_copy(df[:, :, :], dc[:, :, :]))
                    link(nc.vector.tensor_tensor(same[:, :], df[:, 0, :], df[:, 1, :], ALU.is_equal))
                    nc.vector.tensor_tensor(more[:, :], df[:, 0, :], df[:, 2, :], ALU.is_equal).then_inc(s_same, 1)
                    dve.wait_ge(s_same, 1)
                    link(nc.vector.tensor_scalar(fresh[:, :], same[:, :], -1.0, BIG, ALU.add, ALU.mult))
                    link(nc.vector.tensor_scalar(last[:, :], more[:, :], -1.0, 1.0, ALU.mult, ALU.add))
                    link(nc.vector.tensor_tensor_scan(pre[:, :], same[:, :], same[:, :], 1.0, ALU.mult, ALU.min))
                    link(nc.vector.tensor_tensor_scan(suf[:, ::-1], more[:, ::-1], more[:, ::-1], 1.0, ALU.mult, ALU.min))
                    link(nc.vector.tensor_scalar(prefresh[:, :], pre[:, :], -1.0, BIG, ALU.add, ALU.mult))
                    dve.wait_ge(s_ld[3], 16)
                    link(nc.vector.tensor_copy(turn[:, 0, :], sc[:, 0, :]))
                    link(nc.vector.tensor_copy(turn[:, 1, :], df[:, 0, :]))
                    nc.vector.scalar_tensor_tensor(out=turn[:, 2, :], in0=more[:, :], scalar=float(SKIP), in1=df[:, 0, :],
                                                   op0=ALU.mult, op1=ALU.add).then_inc(s_turn, 1)
                    for i, m in enumerate((pre[:, 255:256], prefresh[:, 255:256], suf[:, 0:1])):
                        z = nc.vector.tensor_copy(ends[:, i, :], m.to_broadcast([RQ, HEADS]))
                    z.then_inc(s_ends, 1)
                    dve.wait_ge(s_pb, 1)
                    link(nc.vector.tensor_copy(col[:, 2:3], bank[4][:, 12:13]))
                    dve.wait_ge(s_pt, 1)

                    def slots(n):
                        return bank[n // 2][:, (n % 2) * 256:(n % 2) * 256 + 2 * P].rearrange(
                            "p (s q) -> p s q", s=2)[:, :, 0:RQ]

                    for n, to in enumerate((srci, dsti, lasti, ewp)):
                        link(nc.vector.tensor_copy(to[:, :].rearrange("p (q s) -> p s q", s=2), slots(n)))
                    dve.wait_ge(s_pe, 1)
                    for i in range(3):
                        z = nc.vector.tensor_copy(tmask[:, i, :], bank[2][0:HEADS, i * P:i * P + RQ])
                    link(z)

                @block.tensor
                def _(pe):
                    nc.tensor.matmul(bank[3][:, 0:P], w("w1t"), w("cbd"), start=True, stop=True)
                    nc.tensor.matmul(bank[3][:, P:2 * P], w("w2t"), w("cbd"), start=True, stop=True)
                    nc.tensor.matmul(bank[3][:, 2 * P:2 * P + 132], w("w2t"), w("sel2"), start=True, stop=True)
                    nc.tensor.matmul(bank[4][:, 0:8], w("w1t"), w("al1"), start=True, stop=False)
                    nc.tensor.matmul(bank[4][:, 0:8], w("w1t"), w("al2"), start=False, stop=True)
                    nc.tensor.matmul(bank[4][:, 8:10], w("cbd"), w("vec")[:, B1:B2 + 1], start=True, stop=True)
                    nc.tensor.matmul(bank[4][:, 10:11], w("w2"), vec(ONE), start=True, stop=True).then_inc(s_pw, 1)
                    pe.wait_ge(s_col, 1)
                    nc.tensor.matmul(bank[4][:, 12:13], w("cbd"), bcol[:, :], start=True, stop=True).then_inc(s_pb, 1)
                    pe.wait_ge(s_turn, 1)
                    pe.wait_ge(s_ld[4], 16)
                    for n in range(4):
                        for s in range(2):
                            z = nc.tensor.transpose(bank[n // 2][:, (n % 2) * 256 + s * P:(n % 2) * 256 + s * P + RQ],
                                                    turn[:, n, s * P:(s + 1) * P], ident[0:RQ, 0:RQ])
                    z.then_inc(s_pt, 1)
                    pe.wait_ge(s_ends, 1)
                    for i in range(3):
                        z = nc.tensor.transpose(bank[2][0:HEADS, i * P:i * P + RQ], ends[:, i, :], ident[0:RQ, 0:RQ])
                    z.then_inc(s_pe, 1)
            end_phase()

        v.xw = sb("xw", [P, TILES, 2 * C])
        dense_and_gather(nc, sb, sem, bank, w, vec, v, s_reviews)
        end_phase()
        softmax(nc, sb, sem, bank, v, 1)
        end_phase()
        aggregate1(nc, sb, sem, bank, w, vec, v)
        end_phase()
        v.adc = sb("adc", [RQ, 2, 256])
        gather2(nc, sb, sem, bank, w, vec, v)
        end_phase()
        softmax(nc, sb, sem, bank, v, 2)
        end_phase()
        v.x1r = v.xw[:, :, 0:C]
        aggregate2(nc, sb, sem, bank, w, vec, v)
        end_phase()
        aggregate3(nc, sb, sem, bank, w, vec, v, s_reviews)
        end_phase()


def sort_edges(nc, sb0, sem, end_phase, v, s_reviews):
    CHUNK = EP // 7
    with ExitStack() as ph:
        cur = sb0("sort_cur", [RQ, 2, 256], I32, ph)
        curf = sb0("sort_curf", [RQ, 2, 256], F32, ph)
        down = sb0("sort_down", [RQ, 1], F32, ph)
        flag = v.flag
        s_ld, s_wt, s_c, s_dn, s_sum, s_flag = [sem(n) for n in "s_ld s_wt s_c s_dn s_sum s_flag".split()]
        with nc.Block() as block:
            @block.sync
            def _(sp):
                sp.dma_start(cur[:, 0, :], v.dst[1:1 + EP].rearrange("(q j) -> q j", j=256)).then_inc(s_ld, 16)
                sp.dma_start(cur[:, 1, :], v.dst[2:2 + EP].rearrange("(q j) -> q j", j=256)).then_inc(s_ld, 16)
                sp.dma_start(v.wts[:, :], v.wts_in).then_inc(s_wt, 16)
                sp.wait_ge(s_flag, 1)

            @block.vector
            def _(dve):
                dve.wait_ge(s_ld, 32)
                nc.vector.tensor_copy(curf[:, :, :], cur[:, :, :]).then_inc(s_c, 1)
                dve.wait_ge(s_c, 1)
                nc.vector.tensor_tensor(curf[:, 0, :], curf[:, 0, :], curf[:, 1, :], ALU.is_gt).then_inc(s_c, 1)
                dve.wait_ge(s_c, 2)
                nc.vector.tensor_reduce(down[:, :], curf[:, 0, :], AX.X, ALU.add).then_inc(s_dn, 1)
                dve.wait_ge(s_sum, 1)
                nc.vector.tensor_scalar(flag[:, :], v.bank[0][0:1, 0:1], 1.0, None, ALU.min).then_inc(s_flag, 1)

            @block.tensor
            def _(pe):
                pe.wait_ge(s_wt, 16)
                pe.wait_ge(s_dn, 1)
                nc.tensor.matmul(v.bank[0][0:1, 0:1], down[:, :], v.vec(ONE)[0:RQ, :], start=True, stop=True).then_inc(s_sum, 1)
        end_phase()

        kpi = sb0("sort_kpi", [P, TILES], I32, ph)
        spi = sb0("sort_spi", [P, TILES], I32, ph)
        epi = sb0("sort_epi", [P, TILES], F32, ph)
        kpf = sb0("sort_kpf", [P, TILES], F32, ph)
        ownf = sb0("sort_ownf", [P, TILES], F32, ph)
        own = sb0("sort_own", [P, TILES], I32, ph)
        part = sb0("sort_part", [P, TILES], F32, ph)
        rank = sb0("sort_rank", [P, TILES], F32, ph)
        ranki = sb0("sort_ranki", [P, 2, TILES], I32, ph)
        rowi = sb0("sort_rowi", [P, CHUNK], I32, ph)
        rowf = sb0("sort_rowf", [P, CHUNK], F32, ph)
        numi = sb0("sort_numi", [P, CHUNK], I32, ph)
        numf = sb0("sort_numf", [P, CHUNK], F32, ph)
        less = sb0("sort_less", [P, CHUNK], F32, ph)
        tie = sb0("sort_tie", [P, CHUNK], F32, ph)
        stage = sb0("sort_stage", [P, 4], I32, ph)
        stagef = sb0("sort_stagef", [P, 1], F32, ph)
        stager = sb0("sort_stager", [P, C], F32, ph)
        s_own, s_in, s_row, s_v, s_rank, s_stage, s_rv, s_all, s_cp, s_pad = [sem(n) for n in (
            "s_own s_in s_row s_v s_rank s_stage s_rv s_all s_cp s_pad").split()]
        s_put = [sem(f"s_put{n}") for n in range(4)]

        with nc.Block() as block:
            @block.sync
            def _(sp):
                unsorted = sp.value_load(flag[0:1, 0:1], min_val=0, max_val=1)
                with sp.If(unsorted == 0):
                    sp.dma_start(v.dst_s, v.dst).then_inc(s_cp, 16)
                    sp.dma_start(v.src_s, v.src).then_inc(s_cp, 16)
                    sp.dma_start(v.ew_s, v.ew).then_inc(s_cp, 16)
                    sp.wait_ge(s_cp, 48)
                with sp.Else():
                    sp.dma_start(kpi[:, :], v.dst[1:1 + EP].rearrange("(p t) -> p t", t=TILES)).then_inc(s_in, 16)
                    sp.dma_start(spi[:, :], v.src.rearrange("(p t) -> p t", t=TILES)).then_inc(s_in, 16)
                    sp.dma_start(epi[:, :], v.ew.rearrange("(p t) -> p t", t=TILES)).then_inc(s_in, 16)
                    for c in range(EP // CHUNK):
                        after_apart(sp, s_v, 3 + c * (5 * TILES + 3), v.s_passed)
                        sp.dma_start(rowi[:, :], v.dst[1 + c * CHUNK:1 + (c + 1) * CHUNK].unsqueeze(0).to_broadcast([P, CHUNK])
                                     ).then_inc(s_row, 16)
                    sp.dma_start(v.dst_s[0:1], v.dst[0:1]).then_inc(s_pad, 16)
                    sp.dma_start(v.dst_s[EP + 1:EP + 2], v.dst[EP + 1:EP + 2]).then_inc(s_pad, 16)
                    sp.wait_ge(s_pad, 32)
                    sp.wait_ge(s_all, 1)
                    sp.sem_inc(s_reviews, 16)

            @block.vector
            def _(dve):
                unsorted = dve.value_load(flag[0:1, 0:1], min_val=0, max_val=1)
                with dve.If(unsorted == 1):
                    dve.wait_ge(s_own, 1)
                    dve.wait_ge(s_in, 48)
                    nc.vector.tensor_copy(ownf[:, :], own[:, :])
                    nc.vector.tensor_copy(numf[:, :], numi[:, :]).then_inc(s_v, 1)
                    nc.vector.tensor_copy(kpf[:, :], kpi[:, :]).then_inc(s_v, 1)
                    nc.vector.memset(rank[:, :], 0.0).then_inc(s_v, 1)
                    for c in range(EP // CHUNK):
                        done = 3 + c * (5 * TILES + 3)
                        dve.wait_ge(s_v, done)
                        dve.wait_ge(s_row, 16 * (c + 1))
                        nc.vector.tensor_copy(rowf[:, :], rowi[:, :]).then_inc(s_v, 1)
                        with dve.Fori(0, TILES) as t:
                            one = bass.ds(t, 1)
                            dve.wait_ge(s_v, 5 * t + (done + 1))
                            nc.vector.tensor_scalar(less[:, :], rowf[:, :], kpf[:, one], None, ALU.is_lt).then_inc(s_v, 1)
                            nc.vector.tensor_scalar(tie[:, :], rowf[:, :], kpf[:, one], None, ALU.is_equal).then_inc(s_v, 1)
                            dve.wait_ge(s_v, 5 * t + (done + 3))
                            nc.vector.scalar_tensor_tensor(out=tie[:, :], in0=numf[:, :], scalar=ownf[:, one], in1=tie[:, :],
                                                           op0=ALU.is_lt, op1=ALU.mult).then_inc(s_v, 1)
                            dve.wait_ge(s_v, 5 * t + (done + 4))
                            nc.vector.tensor_tensor(less[:, :], less[:, :], tie[:, :], ALU.add).then_inc(s_v, 1)
                            dve.wait_ge(s_v, 5 * t + (done + 5))
                            nc.vector.tensor_reduce(part[:, one], less[:, :], AX.X, ALU.add).then_inc(s_v, 1)
                        dve.wait_ge(s_v, done + 1 + 5 * TILES)
                        nc.vector.tensor_scalar(numf[:, :], numf[:, :], float(CHUNK), None, ALU.add).then_inc(s_v, 1)
                        nc.vector.tensor_tensor(rank[:, :], rank[:, :], part[:, :], ALU.add).then_inc(s_v, 1)
                    dve.wait_ge(s_v, 3 + (EP // CHUNK) * (5 * TILES + 3))
                    nc.vector.tensor_copy(ranki[:, 0, :], rank[:, :])
                    nc.vector.tensor_scalar(ranki[:, 1, :], rank[:, :], 1.0, None, ALU.add).then_inc(s_rank, 1)

            @block.gpsimd
            def _(pool):
                unsorted = pool.value_load(flag[0:1, 0:1], min_val=0, max_val=1)
                with pool.If(unsorted == 1):
                    pool.iota(own[:, :], pattern=[[1, TILES]], base=0, channel_multiplier=TILES)
                    pool.iota(numi[:, :], pattern=[[1, CHUNK]], base=0, channel_multiplier=0).then_inc(s_own, 1)
                    pool.wait_ge(s_rank, 1)
                    pool.wait_ge(s_in, 48)
                    rows = v.ea.rearrange("(p t) f -> p t f", t=TILES)
                    with pool.Fori(0, TILES) as t:
                        one = bass.ds(t, 1)
                        nc.gpsimd.tensor_copy(stage[:, 0:2], ranki[:, :, one].rearrange("p a b -> p (a b)"))
                        nc.gpsimd.tensor_copy(stage[:, 2:3], kpi[:, one])
                        nc.gpsimd.tensor_copy(stage[:, 3:4], spi[:, one])
                        nc.gpsimd.tensor_copy(stagef[:, :], epi[:, one]).then_inc(s_stage, 1)
                        pool.dma_start(stager[:, :], rows[:, one, :].rearrange("p a f -> p (a f)")).then_inc(s_rv, 16)
                        pool.wait_ge(s_stage, t + 1)
                        after_apart(pool, s_rv, 16 * t + 16, v.s_passed)
                        for n, (to, at, val) in enumerate((
                                (v.src_s.unsqueeze(1), 0, stage[:, 3:4]), (v.dst_s.unsqueeze(1), 1, stage[:, 2:3]),
                                (v.ew_s.unsqueeze(1), 0, stagef[:, :]), (v.ea_s, 0, stager[:, :]))):
                            pool.indirect_dma_start(to, bass.IndirectOffsetOnAxis(ap=stage[:, at:at + 1], axis=0), val, None
                                                    ).then_inc(s_put[n], 16)
                        for n in range(4):
                            pool.wait_ge(s_put[n], 16 * t + 16)
                    pool.sem_inc(s_all, 1)
        end_phase()


def uses(s):
    return 16 * s.half + 16


def dense_and_gather(nc, sb0, sem, bank, w, vec, v, s_reviews):
    ph = ExitStack()

    def sb(name, shape, dt=F32):
        return sb0(name, shape, dt, ph)

    def pair(name):
        return [sem(f"{name}_{j}") for j in range(2)]

    with ph:
        xT = [sb(f"xT{h}", [P, 2, 512]) for h in range(4)]
        y1 = [[sb(f"y1{h}{j}", [P, 512]) for j in range(2)] for h in range(2)]
        a = [[sb(f"a{n}{j}", [P, 512]) for j in range(2)] for n in range(2)]
        b = [[sb(f"b{n}{j}", [P, 512]) for j in range(2)] for n in range(2)]
        g = [[sb(f"g{n}{j}", [P, 512]) for j in range(2)] for n in range(2)]
        sT = [sb(f"sT{j}", [P, 512]) for j in range(2)]
        sqf = [sb(f"sqf{j}", [P, 512]) for j in range(2)]
        yrow = [sb(f"yrow{j}", [P, 512]) for j in range(2)]
        x1row = [sb(f"x1row{j}", [P, 512]) for j in range(2)]
        orow = [sb(f"orow{j}", [P, 512]) for j in range(2)]
        ssum = sb("ssum", [P, 2 * CH])
        logs = sb("logs", [P, 2, 2 * CH])
        scale = sb("scale", [P, 2, 2 * CH])
        xe = [sb(f"xe{h}", [P, 4, 2 * ROW]) for h in range(2)]
        xeT = sb("xeT", [P, 512])
        isrc = [sb(f"isrc{h}", [P, 4], I32) for h in range(2)]
        idst = [sb(f"idst{h}", [P, 4], I32) for h in range(2)]
        p1, p2, pv, pe_, pf = bank[0:2], bank[2:4], bank[4], bank[5], bank[6:8]
        hid = (p1, p2)

        s_x = [sem(f"s_x{h}") for h in range(4)]
        s_is, s_id, s_xe, s_xd, s_yst, s_xst, s_ost = (
            pair(n) for n in "s_is s_id s_xe s_xd s_yst s_xst s_ost".split())
        s_yp, s_yr, s_sT, s_fp, s_fq, s_red, s_x1, s_o = (
            pair(n) for n in "s_yp s_yr s_sT s_fp s_fq s_red s_x1 s_o".split())
        s_h, s_sq, s_var, s_lv, s_rs, s_u, s_e, s_g, s_y = (
            [pair(f"{n}{i}") for i in range(2)] for n in "s_h s_sq s_var s_lv s_rs s_u s_e s_g s_y".split())
        s_ln, s_sc, s_eTp, s_eT, s_cj, s_lgp, s_lg, s_xwp, s_xw = (
            sem(n) for n in "s_ln s_sc s_eTp s_eT s_cj s_lgp s_lg s_xwp s_xw".split())

        def by_node(table):
            return table.rearrange("(d p c) f -> d p (c f)", p=P, c=CH)

        with nc.Block() as block:
            @block.sync
            def _(sp):
                def load_x(s):
                    if s.runs():
                        for j in range(2):
                            after_apart(sp, s_h[0][j], s.k - 3, v.s_passed)
                            after_apart(sp, s_sT[j], s.k - 3, v.s_passed)
                        sp.dma_start(xT[s.rest][:, :, :], v.x[bass.ds(2 * s.k, 2)].rearrange("j p n -> p j n")
                                     ).then_inc(s_x[s.rest], 16)

                def load_indices(s):
                    if s.runs():
                        after_apart(sp, s_xe[s.odd], 128 * s.half, v.s_passed)
                        sp.dma_start(isrc[s.odd][:, :], v.srci[:, bass.ds(4 * s.k, 4)]).then_inc(s_is[s.odd], 16)
                        sp.dma_start(idst[s.odd][:, :], v.dsti[:, bass.ds(4 * s.k, 4)]).then_inc(s_id[s.odd], 16)

                def keep_targets(s):
                    if s.runs():
                        after_apart(sp, s_xe[s.odd], 128 * s.half + 128, v.s_passed)
                        for h in range(2):
                            sp.dma_start(v.xd_d[:, bass.ds(4 * s.k, 4), :].rearrange("p (c h) f -> p h c f", h=2)[:, h],
                                         xe[s.odd][:, 2 * h:2 * h + 2, ROW:ROW + C]).then_inc(s_xd[s.odd], 16)

                def store(s, j, table, rows, written, stored):
                    if s.runs():
                        after_apart(sp, written[j], s.k + 1, v.s_passed)
                        sp.dma_start(by_node(table)[2 * s.k + j], rows[j][:, :]).then_inc(stored[j], 16)

                def body(s):
                    load_indices(s)
                    store(s.back(4), 0, v.out, orow, s_o, s_ost)
                    keep_targets(s.back(1))
                    store(s.back(2), 0, v.y_table, yrow, s_yr, s_yst)
                    store(s.back(4), 0, v.x1_table, x1row, s_x1, s_xst)
                    load_x(s.back(-1))
                    store(s.back(4), 1, v.x1_table, x1row, s_x1, s_xst)
                    store(s.back(4), 1, v.out, orow, s_o, s_ost)
                    store(s.back(2), 1, v.y_table, yrow, s_yr, s_yst)
                load_x(step(0))
                run_steps(sp, body, 4, unroll=4)
                unsorted = sp.value_load(v.flag[0:1, 0:1], min_val=0, max_val=1)
                with sp.If(unsorted == 0):
                    sp.dma_start(v.ea_s.rearrange("(a b) f -> a (b f)", a=P), v.ea.rearrange("(a b) f -> a (b f)", a=P)
                                 ).then_inc(s_reviews, 16)
                for j in range(2):
                    sp.wait_ge(s_yst[j], 16 * STEPS)
                    sp.wait_ge(s_xst[j], 16 * STEPS)
                    sp.wait_ge(s_ost[j], 16 * STEPS)
                sp.wait_ge(s_xd[0], 32 * (STEPS // 2 + 1))
                sp.wait_ge(s_xd[1], 32 * (STEPS // 2))

            @block.gpsimd
            def _(pool):
                def gather(s):
                    if s.runs():
                        after_apart(pool, s_is[s.odd], uses(s), v.s_passed)
                        after_apart(pool, s_id[s.odd], uses(s), v.s_passed)
                        after_apart(pool, s_eTp, s.k - 1, v.s_passed)
                        after_apart(pool, s_cj, s.k - 1, v.s_passed)
                        after_apart(pool, s_xd[s.odd], 32 * s.half, v.s_passed)
                        for t in range(4):
                            for n, (i, rows) in enumerate(((isrc, v.xs), (idst, v.xt))):
                                pool.indirect_dma_start(xe[s.odd][:, t, n * ROW:(n + 1) * ROW], None, rows,
                                                        bass.IndirectOffsetOnAxis(ap=i[s.odd][:, t:t + 1], axis=0)
                                                        ).then_inc(s_xe[s.odd], 16)

                def residual(s, j):
                    if s.runs():
                        after(pool, s_x[s.rest], 16 * s.quarter + 16)
                        after(pool, s_y[1][j], s.k + 1)
                        after(pool, s_fp[j], s.k)
                        nc.gpsimd.tensor_tensor(sT[j][:, :], g[1][j][:, :], xT[s.rest][:, j, :], ALU.add).then_inc(s_sT[j], 1)

                def body(s):
                    gather(s)
                    residual(s.back(2), 1)
                    residual(s.back(2), 0)
                run_steps(pool, body, 2, unroll=4)

            @block.tensor
            def _(pe):
                def layer(n, s, j):
                    if s.runs():
                        if n == 0:
                            after(pe, s_x[s.rest], 16 * s.quarter + 16)
                        else:
                            after(pe, s_y[0][j], s.k + 1)
                        after(pe, s_u[n][j], s.k)
                        nc.tensor.matmul(hid[n][j][:, :], (v.w1c, v.w2c)[n][:, :],
                                         xT[s.rest][:, j, :] if n == 0 else y1[s.odd][j][:, :],
                                         start=True, stop=True).then_inc(s_h[n][j], 1)

                def variance(n, s, j, free, count):
                    if s.runs():
                        after(pe, s_sq[n][j], s.k + 1)
                        after(pe, free, count)
                        nc.tensor.matmul(pv[:, :], w("jbd"), a[n][j][:, :], start=True, stop=True).then_inc(s_var[n][j], 1)

                def y_turn(s, j, free, count):
                    if s.runs():
                        after(pe, free, count)
                        for m in range(4):
                            z = nc.tensor.transpose(pe_[:, m * P:(m + 1) * P], y1[s.odd][j][:, m * P:(m + 1) * P], v.ident)
                        z.then_inc(s_yp[j], 1)

                def final(s, j):
                    if s.runs():
                        after(pe, s_sT[j], s.k + 1)
                        after(pe, s_x1[j], s.k)
                        after(pe, s_o[j], s.k)
                        for m in range(4):
                            z = nc.tensor.matmul(pf[j][:, m * P:(m + 1) * P], sT[j][:, m * P:(m + 1) * P], w("cbd"),
                                                 start=True, stop=True)
                        z.then_inc(s_fp[j], 1)

                def edge_turn(s):
                    if s.runs():
                        after(pe, s_xe[s.odd], 128 * s.half + 128)
                        after(pe, s_yr[0], s.k)
                        for t in range(4):
                            z = nc.tensor.transpose(pe_[:, t * P:(t + 1) * P], xe[s.odd][:, t, 1:1 + 2 * C], v.ident)
                        z.then_inc(s_eTp, 1)

                def edge_logits(s):
                    if s.runs():
                        after(pe, s_eT, s.k + 1)
                        for t in range(4):
                            z = nc.tensor.matmul(pe_[:, t * 8:t * 8 + 8], xeT[:, t * P:(t + 1) * P], v.lgw[:, :],
                                                 start=True, stop=True)
                        z.then_inc(s_lgp, 1)

                def edge_features(s):
                    if s.runs():
                        after(pe, s_lg, s.k + 1)
                        for t in range(4):
                            z = nc.tensor.matmul(pe_[:, t * P:(t + 1) * P], xeT[:, t * P:(t + 1) * P], w("w1"),
                                                 start=True, stop=True)
                        z.then_inc(s_xwp, 1)

                def body(s):
                    e, f = s.back(1), s.back(2)
                    layer(0, s, 0)
                    y_turn(f, 1, *((s_xw, f.k + 2) if e.runs() else (s_yr[0], f.k + 1)))
                    variance(1, e, 0, s_lv[0][1], e.k + 1)
                    layer(1, e, 1)
                    y_turn(e, 0, *((s_xw, 1) if isinstance(s.k, int) and s.k == 1 else (s_yr[1], e.k)))
                    layer(0, s, 1)
                    variance(1, e, 1, s_lv[1][0], e.k + 1)
                    edge_turn(s)
                    variance(0, s, 0, s_lv[1][1], s.k)
                    edge_logits(s)
                    variance(0, s, 1, s_lv[0][0], s.k + 1)
                    final(f, 0)
                    edge_features(s)
                    final(f, 1)
                    layer(1, s, 0)
                run_steps(pe, body, 2, unroll=4)

            @block.scalar
            def _(act):
                act.preload_act_table_set("natural_log_exp_and_others")
                bias = ((v.b1c, vec(BE1)), (v.b2c_dense, vec(BE2)))
                gain = (vec(G1), vec(G2))

                def square(n, s, j):
                    if s.runs():
                        after(act, s_h[n][j], s.k + 1)
                        after(act, s_y[n][j], s.k)
                        nc.scalar.activation(a[n][j][:, :], hid[n][j][:, :], ACT.Square, bias=bias[n][0]
                                             ).then_inc(s_sq[n][j], 1)

                def log_variance(n, s, j):
                    if s.runs():
                        after(act, s_var[n][j], s.k + 1)
                        after(act, s_e[n][j], s.k)
                        after(act, s_g[n][j], s.k)
                        nc.scalar.activation(b[n][j][:, :], pv[:, :], ACT.Ln, bias=vec(EPS)).then_inc(s_lv[n][j], 1)

                def rstd(n, s, j):
                    if s.runs():
                        after(act, s_lv[n][j], s.k + 1)
                        nc.scalar.activation(b[n][j][:, :], b[n][j][:, :], ACT.Exp, scale=-0.5).then_inc(s_rs[n][j], 1)

                def elu_exp(n, s, j):
                    if s.runs():
                        after(act, s_u[n][j], s.k + 1)
                        nc.scalar.activation(a[n][j][:, :], b[n][j][:, :], ACT.Exp, bias=bias[n][1], scale=gain[n]
                                             ).then_inc(s_e[n][j], 1)

                def final_square(s, j):
                    if s.runs():
                        after(act, s_fp[j], s.k + 1)
                        after(act, s_red[j], s.k)
                        nc.scalar.activation(sqf[j][:, :], pf[j][:, :], ACT.Square).then_inc(s_fq[j], 1)

                def final_log(s):
                    if s.runs():
                        after(act, s_red[0], s.k + 1)
                        after(act, s_red[1], s.k + 1)
                        after(act, s_sc, s.k)
                        nc.scalar.activation(logs[:, 0, :], ssum[:, :], ACT.Ln, bias=vec(EPS), scale=1.0 / C)
                        nc.scalar.activation(logs[:, 1, :], ssum[:, :], ACT.Ln, bias=vec(EPS2), scale=(1.0 + LN_EPS) / C
                                             ).then_inc(s_ln, 1)

                def final_exp(s):
                    if s.runs():
                        after(act, s_ln, s.k + 1)
                        for j in range(2):
                            after(act, s_x1[j], s.k)
                            after(act, s_o[j], s.k)
                        nc.scalar.activation(scale[:, :, :], logs[:, :, :], ACT.Exp, scale=-0.5).then_inc(s_sc, 1)

                def edge_copy(s):
                    if s.runs():
                        after(act, s_eTp, s.k + 1)
                        after(act, s_xwp, s.k)
                        nc.scalar.activation(xeT[:, :], pe_[:, :], ACT.Copy).then_inc(s_eT, 1)
                        nc.scalar.activation(v.cjp[:, bass.ds(4 * s.k, 4)], xe[s.odd][:, :, 0], ACT.Copy)
                        nc.scalar.activation(v.cip[:, bass.ds(4 * s.k, 4)], xe[s.odd][:, :, 2 * ROW - 1], ACT.Copy
                                             ).then_inc(s_cj, 1)

                def body(s):
                    e, f = s.back(1), s.back(2)
                    square(0, s, 0)
                    log_variance(1, e, 0)
                    rstd(1, e, 0)
                    square(1, e, 1)
                    final_log(s.back(3))
                    final_exp(s.back(3))
                    square(0, s, 1)
                    log_variance(1, e, 1)
                    edge_copy(s)
                    rstd(1, e, 1)
                    log_variance(0, s, 0)
                    rstd(0, s, 0)
                    elu_exp(1, e, 0)
                    log_variance(0, s, 1)
                    elu_exp(0, s, 0)
                    rstd(0, s, 1)
                    elu_exp(1, e, 1)
                    final_square(f, 0)
                    elu_exp(0, s, 1)
                    square(1, s, 0)
                    final_square(f, 1)
                run_steps(act, body, 3)

            @block.vector
            def _(dve):
                shift = (v.b1c, v.b2c_dense)
                gain = ((vec(G1), v.be1p), (vec(G2), v.be2p))

                def norm(n, s, j):
                    if s.runs():
                        after(dve, s_rs[n][j], s.k + 1)
                        nc.vector.scalar_tensor_tensor(out=b[n][j][:, :], in0=hid[n][j][:, :], scalar=shift[n],
                                                       in1=b[n][j][:, :], op0=ALU.add, op1=ALU.mult).then_inc(s_u[n][j], 1)

                def line(n, s, j):
                    if s.runs():
                        after(dve, s_u[n][j], s.k + 1)
                        after(dve, (s_y[0], s_sT)[n][j], s.k)
                        nc.vector.tensor_scalar(g[n][j][:, :], b[n][j][:, :], gain[n][0], gain[n][1], ALU.mult, ALU.add
                                                ).then_inc(s_g[n][j], 1)

                def elu(n, s, j):
                    if s.runs():
                        after(dve, s_e[n][j], s.k + 1)
                        after(dve, s_g[n][j], s.k + 1)
                        if n == 0:
                            after(dve, s_h[1][j], s.k - 1)
                            after(dve, s_yp[j], s.k - 1)
                        to = y1[s.odd][j] if n == 0 else g[1][j]
                        nc.vector.scalar_tensor_tensor(out=to[:, :], in0=a[n][j][:, :], scalar=1.0, in1=g[n][j][:, :],
                                                       op0=ALU.min, op1=ALU.max).then_inc(s_y[n][j], 1)

                def y_rows(s, j):
                    if s.runs():
                        after(dve, s_yp[j], s.k + 1)
                        after(dve, s_yst[j], 16 * s.k)
                        nc.vector.tensor_scalar(yrow[j][:, :], pe_[:, :], -1.0, None, ALU.add).then_inc(s_yr[j], 1)

                def reduce(s, j):
                    if s.runs():
                        after(dve, s_fq[j], s.k + 1)
                        after(dve, s_ln, s.k)
                        nc.vector.tensor_reduce(ssum[:, j * CH:(j + 1) * CH], sqf[j][:, :].rearrange("p (c f) -> p c f", f=C),
                                                AX.X, ALU.add).then_inc(s_red[j], 1)

                def rows(s, j, i, to, stored, done):
                    if s.runs():
                        after(dve, s_sc, s.k + 1)
                        after(dve, stored[j], 16 * s.k)
                        nc.vector.tensor_tensor(
                            to[j][:, :].rearrange("p (c f) -> p c f", f=C), pf[j][:, :].rearrange("p (c f) -> p c f", f=C),
                            scale[:, i, j * CH:(j + 1) * CH].unsqueeze(2).to_broadcast([P, CH, C]), ALU.mult
                        ).then_inc(done[j], 1)

                def edge_logits(s):
                    if s.runs():
                        after(dve, s_lgp, s.k + 1)
                        nc.vector.tensor_copy(v.lg[:, bass.ds(4 * s.k, 4), :],
                                              pe_[:, 0:32].rearrange("p (t n) -> p t n", n=8)).then_inc(s_lg, 1)

                def edge_features(s):
                    if s.runs():
                        after(dve, s_xwp, s.k + 1)
                        nc.vector.tensor_copy(v.xw[:, bass.ds(4 * s.k, 4), :],
                                              pe_[:, :].rearrange("p (t n) -> p t n", n=2 * C)).then_inc(s_xw, 1)

                def body(s):
                    e, f = s.back(1), s.back(2)
                    norm(0, s, 0)
                    edge_logits(s)
                    line(0, s, 0)
                    elu(1, e, 0)
                    elu(0, s, 0)
                    norm(0, s, 1)
                    edge_features(s)
                    line(0, s, 1)
                    line(1, e, 1)
                    elu(0, s, 1)
                    elu(1, e, 1)
                    y_rows(e, 1)
                    reduce(f, 0)
                    reduce(f, 1)
                    y_rows(s, 0)
                    norm(1, s, 0)
                    rows(f, 0, 1, orow, s_ost, s_o)
                    rows(f, 0, 0, x1row, s_xst, s_x1)
                    rows(f, 1, 0, x1row, s_xst, s_x1)
                    rows(f, 1, 1, orow, s_ost, s_o)
                    line(1, s, 0)
                    norm(1, s, 1)
                run_steps(dve, body, 2)


class Rows:

    def __init__(self, nc, v, bank, sb, s_chain, s_rows, s_turned):
        self.nc, self.v, self.bank = nc, v, bank
        self.s_chain, self.s_rows, self.s_turned = s_chain, s_rows, s_turned
        self.links = self.rounds = 0
        self.turns = 0
        self.carry = sb("carry", [HEADS, 2, RQ + 1])

    def link(self, ins):
        self.links += 1
        ins.then_inc(self.s_chain, 1)
        self.nc.vector.wait_ge(self.s_chain, self.links)

    def turned(self, ins):
        self.rounds += 1
        ins.then_inc(self.s_rows, 1)
        self.nc.vector.wait_ge(self.s_turned, self.rounds)

    def _carry(self, heads, mask, op0, op1, first, backward):
        nc, c = self.nc, self.carry[0:heads, 0, :]
        turned = self.bank[6][0:heads, 0:RQ]
        m = self.v.tmask[0:heads, mask, :]
        if backward:
            self.link(nc.vector.memset(c[:, RQ:RQ + 1], first))
            ins = nc.vector.tensor_tensor_scan(c[:, 0:RQ][:, ::-1], m[:, ::-1], turned[:, ::-1], first, op0, op1)
        else:
            self.link(nc.vector.memset(c[:, 0:1], first))
            ins = nc.vector.tensor_tensor_scan(c[:, 1:RQ + 1], m, turned, first, op0, op1)
        self.turned(ins)

    def forward(self, x, of, heads, largest):
        nc, v = self.nc, self.v
        inner, outer, mask, op0, op1, first = (
            (v.fresh, v.prefresh, 1, ALU.add, ALU.max, -BIG) if largest else (v.same, v.pre, 0, ALU.mult, ALU.add, 0.0))
        for h in range(heads):
            ins = nc.vector.tensor_tensor_scan(x[:, h, :], inner[:, :], of[:, h, :], first, op0, op1)
        self.turned(ins)
        self._carry(heads, mask, op0, op1, first, False)
        for h in range(heads):
            ins = nc.vector.scalar_tensor_tensor(out=x[:, h, :], in0=outer[:, :], scalar=self.bank[7][0:RQ, h:h + 1],
                                                 in1=x[:, h, :], op0=op0, op1=op1)
        self.link(ins)

    def spread(self, x, heads):
        nc, v = self.nc, self.v
        for h in range(heads):
            ins = nc.vector.tensor_tensor(x[:, h, :], x[:, h, :], v.last[:, :], ALU.mult)
        self.link(ins)
        for h in range(heads):
            ins = nc.vector.tensor_tensor_scan(x[:, h, ::-1], v.more[:, ::-1], x[:, h, ::-1], 0.0, ALU.mult, ALU.add)
        self.turned(ins)
        self._carry(heads, 2, ALU.mult, ALU.add, 0.0, True)
        for h in range(heads):
            ins = nc.vector.scalar_tensor_tensor(out=x[:, h, :], in0=v.suf[:, :], scalar=self.bank[7][0:RQ, h:h + 1],
                                                 in1=x[:, h, :], op0=ALU.mult, op1=ALU.add)
        self.link(ins)

    def turn(self, x, heads, backward):
        nc, v, c = self.nc, self.v, self.carry
        end = 0 if backward else 255
        self.turns += 1
        nc.tensor.wait_ge(self.s_rows, self.turns)
        nc.tensor.transpose(self.bank[6][0:heads, 0:RQ], x[:, 0:heads, end], v.ident[0:RQ, 0:RQ]).then_inc(self.s_turned, 1)
        self.turns += 1
        nc.tensor.wait_ge(self.s_rows, self.turns)
        at = 1 if backward else 0
        nc.tensor.transpose(self.bank[7][0:RQ, 0:heads], c[0:heads, 0, at:at + RQ], v.ident[0:heads, 0:heads]
                            ).then_inc(self.s_turned, 1)


def softmax(nc, sb0, sem, bank, v, layer):
    H = HEADS if layer == 1 else 1
    ph = ExitStack()

    def sb(name, shape, dt=F32):
        return sb0(f"{name}{layer}", shape, dt, ph)

    with ph:
        z = sb("z", [RQ, 2 * H, 256])
        top = sb("top", [RQ, H, 256])
        den = sb("den", [RQ, H, 256])
        s_turn, s_raw, s_chain, s_rows, s_turned, s_d, s_exp, s_w, s_back, s_out, s_loops = [sem(n) for n in (
            "s_turn s_raw s_chain s_rows s_turned s_d s_exp s_w s_back s_out s_loops").split()]
        rows = Rows(nc, v, bank, sb, s_chain, s_rows, s_turned)
        per = min(2, H)
        sources = 2 * H if layer == 1 else 1
        first = 0 if layer == 1 else 2

        def half(n, s):
            return bank[n // 2][0:RQ, (n % 2) * 256 + s * P:(n % 2) * 256 + (s + 1) * P]

        def slot(n, s):
            return slots(n)[:, s, :]

        def slots(n):
            at = n % per * 256
            return bank[n // per][:, at:at + 256].rearrange("p (s q) -> p s q", s=2)[:, :, 0:RQ]

        with nc.Block() as block:
            @block.tensor
            def _(pe):
                for n in range(sources):
                    for s in range(2):
                        t = nc.tensor.transpose(half(n, s), v.lg[:, s::2, first + n], v.ident)
                t.then_inc(s_turn, 1)
                rows.turn(top, H, False)
                rows.turn(top, H, True)
                rows.turn(den, H, False)
                rows.turn(den, H, True)
                pe.wait_ge(s_w, 1)
                for n in range(2 * H):
                    for s in range(2):
                        t = nc.tensor.transpose(slot(n, s), z[:, n, s * P:(s + 1) * P], v.ident[0:RQ, 0:RQ])
                t.then_inc(s_back, 1)

            @block.scalar
            def _(act):
                act.preload_act_table_set("natural_log_exp_and_others")
                act.wait_ge(s_turn, 1)
                for b in range(-(-sources // 2)):
                    k = min(2, sources - 2 * b)
                    t = nc.scalar.activation(z[:, 2 * b:2 * b + k, :], bank[b][0:RQ, 0:256 * k].rearrange(
                        "p (n j) -> p n j", j=256), ACT.Copy)
                t.then_inc(s_raw, 1)
                act.wait_ge(s_d, 1)
                nc.scalar.activation(z[:, :, :], z[:, :, :], ACT.Exp).then_inc(s_exp, 1)
                act.wait_ge(s_back, 1)
                for n in range(H, 2 * H):
                    t = nc.scalar.activation(v.att[:, :, n].rearrange("p (q s) -> p s q", s=2), slots(n), ACT.Copy)
                t.then_inc(s_loops, 1)
                act.wait_ge(s_loops, 1)

            @block.vector
            def _(dve):
                link = rows.link
                dve.wait_ge(s_raw, 1)
                if layer == 2:
                    link(nc.vector.tensor_tensor(z[:, 0, :], z[:, 0, :], v.adc[:, 0, :], ALU.add))
                    link(nc.vector.tensor_copy(z[:, 1, :], v.adc[:, 1, :]))
                k = 2 * H if layer == 1 else 1
                link(nc.vector.scalar_tensor_tensor(out=z[:, 0:k, :], in0=z[:, 0:k, :], scalar=SLOPE, in1=z[:, 0:k, :],
                                                    op0=ALU.mult, op1=ALU.max))
                rows.forward(top, z, H, True)
                rows.spread(top, H)
                link(nc.vector.tensor_tensor(top[:, :, :], top[:, :, :], z[:, H:2 * H, :], ALU.max))
                nc.vector.tensor_tensor(z[:, 0:H, :], z[:, 0:H, :], top[:, :, :], ALU.subtract)
                nc.vector.tensor_tensor(z[:, H:2 * H, :], z[:, H:2 * H, :], top[:, :, :], ALU.subtract).then_inc(s_d, 1)
                dve.wait_ge(s_exp, 1)
                rows.forward(den, z, H, False)
                rows.spread(den, H)
                link(nc.vector.scalar_tensor_tensor(out=den[:, :, :], in0=den[:, :, :], scalar=SM_EPS, in1=z[:, H:2 * H, :],
                                                    op0=ALU.add, op1=ALU.add))
                link(nc.vector.reciprocal(den[:, :, :], den[:, :, :]))
                nc.vector.tensor_tensor(z[:, 0:H, :], z[:, 0:H, :], den[:, :, :], ALU.mult)
                link(nc.vector.tensor_tensor(z[:, H:2 * H, :], z[:, H:2 * H, :], den[:, :, :], ALU.mult))
                for h in range(H, 2 * H):
                    t = nc.vector.tensor_tensor(z[:, h, :], z[:, h, :], v.last[:, :], ALU.mult)
                t.then_inc(s_w, 1)
                dve.wait_ge(s_back, 1)
                for n in range(H):
                    t = nc.vector.tensor_copy(v.att[:, :, n].rearrange("p (q s) -> p s q", s=2), slots(n))
                t.then_inc(s_out, 1)
                dve.wait_ge(s_out, 1)


def aggregate1(nc, sb0, sem, bank, w, vec, v):
    ph = ExitStack()

    def sb(name, shape, dt=F32):
        return sb0(name + "_a1", shape, dt, ph)

    with ph:
        both = [sb(f"both{h}", [P, 4, 2, C]) for h in range(2)]
        msg = [sb(f"msg{h}", [P, 4, C]) for h in range(2)]
        keep = [sb(f"keep{h}", [C, 512]) for h in range(2)]
        run = [sb(f"run{h}", [C, 512]) for h in range(2)]
        a = [sb(f"a{h}", [P, 256]) for h in range(2)]
        b = [sb(f"b{h}", [P, 256]) for h in range(2)]
        g = sb("g", [P, 256])
        yT = [sb(f"yT{h}", [P, 256]) for h in range(2)]
        yrow = [sb(f"yrow{h}", [P, 4, C]) for h in range(2)]
        ilast = [sb(f"ilast{h}", [P, 4], I32) for h in range(2)]
        s_keep, s_il, s_sc = ([sem(f"{n}{h}") for h in range(2)] for n in ("s_keep", "s_il", "s_sc"))
        (s_both, s_msg, s_fp, s_run, s_h, s_sq, s_var, s_ln, s_rs, s_u, s_e, s_g, s_y, s_yT, s_yp, s_yr, s_xp, s_xc
         ) = [sem(n) for n in "s_both s_msg s_fp s_run s_h s_sq s_var s_ln s_rs s_u s_e s_g s_y s_yT s_yp s_yr s_xp s_xc".split()]

        with nc.Block() as block:
            @block.sync
            def _(sp):
                def load(s):
                    if s.runs():
                        after_apart(sp, s_run, s.k - 1, v.s_passed)
                        sp.dma_start(keep[s.odd][:, :], v.same_d[bass.ds(512 * s.k, 512)].unsqueeze(0).to_broadcast([C, 512])
                                     ).then_inc(s_keep[s.odd], 16)

                def load_last(s):
                    if s.runs():
                        after_apart(sp, s_sc[s.odd], 64 * s.half, v.s_passed)
                        sp.dma_start(ilast[s.odd][:, :], v.lasti[:, bass.ds(4 * s.k, 4)]).then_inc(s_il[s.odd], 16)

                def body(s):
                    load(s.back(-1))
                    load_last(s.back(2))
                load(step(0))
                run_steps(sp, body, 3)

            @block.gpsimd
            def _(pool):
                def put(s):
                    if s.runs():
                        after_apart(pool, s_il[s.odd], uses(s), v.s_passed)
                        after_apart(pool, s_yr, s.k + 1, v.s_passed)
                        for t in range(4):
                            pool.indirect_dma_start(v.y_table, bass.IndirectOffsetOnAxis(ap=ilast[s.odd][:, t:t + 1], axis=0),
                                                    yrow[s.odd][:, t, :], None, bounds_check=NP - 1, oob_is_err=False
                                                    ).then_inc(s_sc[s.odd], 16)
                run_steps(pool, lambda s: put(s.back(3)), 3)
                pool.wait_ge(s_sc[0], 64 * (STEPS // 2 + 1))
                pool.wait_ge(s_sc[1], 64 * (STEPS // 2))

            @block.tensor
            def _(pe):
                def state_turn(s):
                    if s.runs():
                        after(pe, s_yT, s.k + 1)
                        after(pe, s_yr, s.k)
                        for c in range(2):
                            t = nc.tensor.transpose(bank[5][:, c * P:(c + 1) * P], yT[s.odd][:, c * P:(c + 1) * P], v.ident)
                        t.then_inc(s_yp, 1)

                def features(s):
                    if s.runs():
                        after(pe, s_xc, s.k)
                        for c in range(2):
                            t = nc.tensor.matmul(bank[6][:, c * 132:(c + 1) * 132], yT[s.odd][:, c * P:(c + 1) * P],
                                                 v.r2[:, :], start=True, stop=True)
                        t.then_inc(s_xp, 1)

                def body(s):
                    features(s.back(3))
                    variance(nc, pe, s.back(1), bank, w, a, s_sq, s_ln, s_var)
                    message_turn(nc, pe, s, bank, msg, v, s_msg, s_run, s_fp)
                    centre_halves(nc, pe, s, bank, w, run, s_run, s_u, s_h)
                    state_turn(s.back(2))
                run_steps(pe, body, 3)

            @block.scalar
            def _(act):
                act.preload_act_table_set("natural_log_exp_and_others")

                def rows(s):
                    if s.runs():
                        after(act, s_yp, s.k + 1)
                        after(act, s_sc[s.odd], 64 * s.half)
                        for c in range(2):
                            z = nc.scalar.activation(yrow[s.odd][:, c::2, :], bank[5][:, c * P:(c + 1) * P].rearrange(
                                "p (h f) -> p h f", h=2), ACT.Copy)
                        z.then_inc(s_yr, 1)

                def features(s):
                    if s.runs():
                        after(act, s_xp, s.k + 1)
                        tiles = v.xw[:, bass.ds(4 * s.k, 4), :]
                        logit = v.lg[:, bass.ds(4 * s.k, 4), :]
                        for c in range(2):
                            from_ = bank[6][:, c * 132:(c + 1) * 132].rearrange("p (h n) -> p h n", h=2)
                            nc.scalar.activation(tiles[:, c::2, C:2 * C], from_[:, :, 0:C], ACT.Copy)
                            z = nc.scalar.activation(logit[:, c::2, 0:2], from_[:, :, C:C + 2], ACT.Copy)
                        z.then_inc(s_xc, 1)

                def body(s):
                    squares(nc, act, s.back(1), bank, a, v.b1c, s_h, s_y, s_sq)
                    elu_exp(nc, act, s.back(2), a, b, vec(G1), vec(BE1), s_u, s_e)
                    rows(s.back(3))
                    features(s.back(3))
                    norm_scale(nc, act, s.back(1), bank, b, vec(EPS), s_g, s_e, s_var, s_ln, s_rs)
                run_steps(act, body, 3)

            @block.vector
            def _(dve):
                def messages(s):
                    if s.runs():
                        after(dve, s_msg, s.k - 1)
                        nc.vector.tensor_tensor(
                            both[s.odd][:, :, :, :].rearrange("p t n (h c) -> p (t n h) c", h=HEADS),
                            v.xw[:, bass.ds(4 * s.k, 4), :].rearrange("p t (n c) -> p (t n) c", c=C // HEADS),
                            v.att[:, bass.ds(4 * s.k, 4), :].rearrange("p t n -> p (t n)").unsqueeze(2).to_broadcast(
                                [P, 32, C // HEADS]), ALU.mult).then_inc(s_both, 1)

                def minus_one(s):
                    if s.runs():
                        after(dve, s_y, s.k + 1)
                        nc.vector.tensor_scalar(yT[s.odd][:, :], yT[s.odd][:, :], -1.0, None, ALU.add).then_inc(s_yT, 1)

                def body(s):
                    messages(s)
                    message_sum(nc, dve, s, both, msg, s_both, s_fp, s_msg)
                    elu_line(nc, dve, s.back(2), b, g, vec(G1), v.be1p, s_u, s_y, s_g)
                    elu_rows(nc, dve, s.back(2), a, g, yT, s_e, s_g, s_y, s_xp)
                    minus_one(s.back(2))
                    segment_scan(nc, dve, s, bank, keep, run, s_keep, s_fp, s_h, s_run)
                    norm_apply(nc, dve, s.back(1), bank, b, v.b1c, s_rs, s_u)
                run_steps(dve, body, 2)


def centre_halves(nc, pe, s, bank, w, run, s_run, s_u, s_h):
    if s.runs():
        after(pe, s_run, s.k + 1)
        after(pe, s_u, s.k - 1)
        nc.tensor.matmul(bank[2 + s.odd][:, 0:256], w("clo", C), run[s.odd][:, 0:256], start=True, stop=False)
        nc.tensor.matmul(bank[2 + s.odd][:, 0:256], w("chi", C), run[s.odd][:, 256:512], start=False, stop=True).then_inc(s_h, 1)


def message_sum(nc, dve, s, both, msg, s_both, s_fp, s_msg):
    if s.runs():
        after(dve, s_both, s.k + 1)
        after(dve, s_fp, s.k - 1)
        nc.vector.tensor_tensor(msg[s.odd][:, :, :], both[s.odd][:, :, 0, :], both[s.odd][:, :, 1, :], ALU.add
                                ).then_inc(s_msg, 1)


def message_turn(nc, pe, s, bank, msg, v, s_msg, s_run, s_fp):
    if s.runs():
        after(pe, s_msg, s.k + 1)
        after_apart(pe, s_run, s.k - 1, v.s_passed)
        for t in range(4):
            z = nc.tensor.transpose(bank[s.odd][0:C, t * P:(t + 1) * P], msg[s.odd][:, t, :], v.ident)
        z.then_inc(s_fp, 1)


def segment_scan(nc, dve, s, bank, keep, run, s_keep, s_fp, s_h, s_run):
    if s.runs():
        after(dve, s_keep[s.odd], uses(s))
        after(dve, s_fp, s.k + 1)
        after(dve, s_h, s.k - 1)
        after(dve, s_run, s.k)
        carry = 0.0 if isinstance(s.k, int) and s.k == 0 else run[1 - s.odd][:, 511:512]
        nc.vector.tensor_tensor_scan(run[s.odd][:, :], keep[s.odd][:, :], bank[s.odd][0:C, :], carry, ALU.mult, ALU.add
                                     ).then_inc(s_run, 1)


def squares(nc, act, s, bank, a, shift, s_h, s_y, s_sq):
    if s.runs():
        after(act, s_h, s.k + 1)
        after(act, s_y, s.k - 1)
        nc.scalar.activation(a[s.odd][:, :], bank[2 + s.odd][:, 0:256], ACT.Square, bias=shift).then_inc(s_sq, 1)


def variance(nc, pe, s, bank, w, a, s_sq, s_ln, s_var):
    if s.runs():
        after(pe, s_sq, s.k + 1)
        after(pe, s_ln, s.k)
        nc.tensor.matmul(bank[4][:, 0:256], w("jbd"), a[s.odd][:, :], start=True, stop=True).then_inc(s_var, 1)


def norm_scale(nc, act, s, bank, b, eps, s_g, s_e, s_var, s_ln, s_rs):
    if s.runs():
        after(act, s_var, s.k + 1)
        after(act, s_g, s.k - 1)
        after(act, s_e, s.k - 1)
        nc.scalar.activation(b[s.odd][:, :], bank[4][:, 0:256], ACT.Ln, bias=eps).then_inc(s_ln, 1)
        after(act, s_ln, s.k + 1)
        nc.scalar.activation(b[s.odd][:, :], b[s.odd][:, :], ACT.Exp, scale=-0.5).then_inc(s_rs, 1)


def norm_apply(nc, dve, s, bank, b, shift, s_rs, s_u):
    if s.runs():
        after(dve, s_rs, s.k + 1)
        nc.vector.scalar_tensor_tensor(out=b[s.odd][:, :], in0=bank[2 + s.odd][:, 0:256], scalar=shift, in1=b[s.odd][:, :],
                                       op0=ALU.add, op1=ALU.mult).then_inc(s_u, 1)


def elu_exp(nc, act, s, a, b, gain, shift, s_u, s_e):
    if s.runs():
        after(act, s_u, s.k + 1)
        nc.scalar.activation(a[s.odd][:, :], b[s.odd][:, :], ACT.Exp, bias=shift, scale=gain).then_inc(s_e, 1)


def elu_line(nc, dve, s, b, g, gain, shift, s_u, s_y, s_g):
    if s.runs():
        after(dve, s_u, s.k + 1)
        after(dve, s_y, s.k)
        nc.vector.tensor_scalar(g[:, :], b[s.odd][:, :], gain, shift, ALU.mult, ALU.add).then_inc(s_g, 1)


def elu_rows(nc, dve, s, a, g, to, s_e, s_g, s_y, s_read):
    if s.runs():
        after(dve, s_e, s.k + 1)
        after(dve, s_g, s.k + 1)
        after(dve, s_read, s.k - 1)
        nc.vector.scalar_tensor_tensor(out=to[s.odd][:, :], in0=a[s.odd][:, :], scalar=1.0, in1=g[:, :],
                                       op0=ALU.min, op1=ALU.max).then_inc(s_y, 1)


def gather2(nc, sb0, sem, bank, w, vec, v):
    ph = ExitStack()

    def sb(name, shape, dt=F32):
        return sb0(name + "_g2", shape, dt, ph)

    with ph:
        got = [sb(f"got{h}", [P, 4, C]) for h in range(2)]
        gotT = [sb(f"gotT{h}", [P, 256]) for h in range(2)]
        isrc = [sb(f"isrc{h}", [P, 4], I32) for h in range(2)]
        zc = sb("zc", [RQ, 2, 256])
        s_is, s_ga = ([sem(f"{n}{h}") for h in range(2)] for n in ("s_is", "s_ga"))
        s_turn, s_raw, s_chain, s_rows, s_turned, s_tp, s_t, s_xp, s_xc = [sem(n) for n in (
            "s_turn s_raw s_chain s_rows s_turned s_tp s_t s_xp s_xc").split()]
        rows = Rows(nc, v, bank, sb, s_chain, s_rows, s_turned)

        with nc.Block() as block:
            @block.sync
            def _(sp):
                def load(s):
                    if s.runs():
                        after_apart(sp, s_ga[s.odd], 64 * s.half, v.s_passed)
                        sp.dma_start(isrc[s.odd][:, :], v.srci[:, bass.ds(4 * s.k, 4)]).then_inc(s_is[s.odd], 16)
                load(step(0))
                run_steps(sp, lambda s: load(s.back(-1)), 2)

            @block.gpsimd
            def _(pool):
                def body(s):
                    if s.runs():
                        after_apart(pool, s_is[s.odd], uses(s), v.s_passed)
                        after_apart(pool, s_tp, s.k - 1, v.s_passed)
                        for t in range(4):
                            pool.indirect_dma_start(got[s.odd][:, t, :], None, v.y_table,
                                                    bass.IndirectOffsetOnAxis(ap=isrc[s.odd][:, t:t + 1], axis=0)
                                                    ).then_inc(s_ga[s.odd], 16)
                run_steps(pool, body, 1)

            @block.tensor
            def _(pe):
                for n in range(2):
                    for s in range(2):
                        t = nc.tensor.transpose(bank[5][0:RQ, n * 256 + s * P:n * 256 + (s + 1) * P], v.lg[:, s::2, n], v.ident)
                t.then_inc(s_turn, 1)
                rows.turn(v.adc, 2, True)

                def body(s):
                    e = s.back(1)
                    if s.runs():
                        after(pe, s_ga[s.odd], 64 * s.half + 64)
                        after(pe, s_t, s.k - 1)
                        for c in range(2):
                            t = nc.tensor.transpose(bank[s.odd][:, c * P:(c + 1) * P],
                                                    got[s.odd][:, 2 * c:2 * c + 2, :].rearrange("p t f -> p (t f)"), v.ident)
                        t.then_inc(s_tp, 1)
                    if e.runs():
                        after(pe, s_t, e.k + 1)
                        after(pe, s_xc, e.k - 1)
                        for c in range(2):
                            t = nc.tensor.matmul(bank[2 + e.odd][:, c * 132:(c + 1) * 132], gotT[e.odd][:, c * P:(c + 1) * P],
                                                 v.r2[:, :], start=True, stop=True)
                        t.then_inc(s_xp, 1)
                run_steps(pe, body, 1)

            @block.scalar
            def _(act):
                act.preload_act_table_set("natural_log_exp_and_others")

                def body(s):
                    e = s.back(1)
                    if e.runs():
                        after(act, s_xp, e.k + 1)
                        nc.scalar.activation(v.xw[:, bass.ds(4 * e.k, 4), 0:C], bank[2 + e.odd][:, 0:264].rearrange(
                            "p (t n) -> p t n", n=66)[:, :, 0:C], ACT.Copy)
                        nc.scalar.activation(v.lg[:, bass.ds(4 * e.k, 4), 2], bank[2 + e.odd][:, 0:264].rearrange(
                            "p (t n) -> p t n", n=66)[:, :, C], ACT.Copy).then_inc(s_xc, 1)
                    if s.runs():
                        after(act, s_tp, s.k + 1)
                        after(act, s_xp, s.k - 1)
                        nc.scalar.activation(gotT[s.odd][:, :], bank[s.odd][:, 0:256], ACT.Copy).then_inc(s_t, 1)
                run_steps(act, body, 1)

            @block.vector
            def _(dve):
                link = rows.link
                dve.wait_ge(s_turn, 1)
                link(nc.vector.tensor_copy(zc[:, :, :], bank[5][0:RQ, :].rearrange("p (n j) -> p n j", j=256)))
                link(nc.vector.tensor_copy(v.adc[:, 0, :], zc[:, 1, :]))
                link(nc.vector.tensor_tensor(v.adc[:, 1, :], zc[:, 0, :], zc[:, 1, :], ALU.add))
                link(nc.vector.scalar_tensor_tensor(out=v.adc[:, 1, :], in0=v.adc[:, 1, :], scalar=SLOPE,
                                                    in1=v.adc[:, 1, :], op0=ALU.mult, op1=ALU.max))
                rows.spread(v.adc, 2)


def aggregate2(nc, sb0, sem, bank, w, vec, v):
    ph = ExitStack()

    def sb(name, shape, dt=F32):
        return sb0(name + "_a2", shape, dt, ph)

    with ph:
        both = [sb(f"both{h}", [P, 4, 2, C]) for h in range(2)]
        msg = [sb(f"msg{h}", [P, 4, C]) for h in range(2)]
        keep = [sb(f"keep{h}", [C, 512]) for h in range(2)]
        run = [sb(f"run{h}", [C, 512]) for h in range(2)]
        a = [sb(f"a{h}", [P, 256]) for h in range(2)]
        b = [sb(f"b{h}", [P, 256]) for h in range(2)]
        g = sb("g", [P, 256])
        zT = [sb(f"zT{h}", [P, 256]) for h in range(2)]
        sT = [sb(f"sT{h}", [P, 256]) for h in range(2)]
        xd = [sb(f"xd{h}", [P, 4 * C]) for h in range(2)]
        sqf = sb("sqf", [P, 256])
        ssum = sb("ssum", [P, 4])
        logs = sb("logs", [P, 4])
        scale = sb("scale", [P, 4])
        xrow = [sb(f"xrow{h}", [P, 4, C]) for h in range(2)]
        ilast = [sb(f"ilast{h}", [P, 4], I32) for h in range(2)]
        s_keep, s_il, s_sc, s_xd = ([sem(f"{n}{h}") for h in range(2)] for n in ("s_keep", "s_il", "s_sc", "s_xd"))
        (s_both, s_msg, s_fp, s_run, s_h, s_sq, s_var, s_ln, s_rs, s_u, s_e, s_g, s_y, s_xp, s_sT, s_cp, s_fq, s_red,
         s_lf, s_sf, s_x1, s_x1r) = [sem(n) for n in (
             "s_both s_msg s_fp s_run s_h s_sq s_var s_ln s_rs s_u s_e s_g s_y s_xp s_sT s_cp s_fq s_red "
             "s_lf s_sf s_x1 s_x1r").split()]

        with nc.Block() as block:
            @block.sync
            def _(sp):
                def load(s):
                    if s.runs():
                        after_apart(sp, s_run, s.k - 1, v.s_passed)
                        sp.dma_start(keep[s.odd][:, :], v.same_d[bass.ds(512 * s.k, 512)].unsqueeze(0).to_broadcast([C, 512])
                                     ).then_inc(s_keep[s.odd], 16)
                        after_apart(sp, s_xp, s.k - 1, v.s_passed)
                        sp.dma_start(xd[s.odd][:, :], v.xd_d[:, bass.ds(4 * s.k, 4), :].rearrange("p t f -> p (t f)")
                                     ).then_inc(s_xd[s.odd], 16)

                def load_last(s):
                    if s.runs():
                        after_apart(sp, s_sc[s.odd], 64 * s.half, v.s_passed)
                        sp.dma_start(ilast[s.odd][:, :], v.lasti[:, bass.ds(4 * s.k, 4)]).then_inc(s_il[s.odd], 16)

                def body(s):
                    load(s.back(-1))
                    load_last(s.back(2))
                load(step(0))
                run_steps(sp, body, 3)

            @block.gpsimd
            def _(pool):
                def put(s):
                    if s.runs():
                        after_apart(pool, s_il[s.odd], uses(s), v.s_passed)
                        after_apart(pool, s_x1, s.k + 1, v.s_passed)
                        for t in range(4):
                            pool.indirect_dma_start(v.x1_table, bass.IndirectOffsetOnAxis(ap=ilast[s.odd][:, t:t + 1], axis=0),
                                                    xrow[s.odd][:, t, :], None, bounds_check=NP - 1, oob_is_err=False
                                                    ).then_inc(s_sc[s.odd], 16)
                run_steps(pool, lambda s: put(s.back(3)), 3)
                pool.wait_ge(s_sc[0], 64 * (STEPS // 2 + 1))
                pool.wait_ge(s_sc[1], 64 * (STEPS // 2))

            @block.tensor
            def _(pe):
                def centre_rows(s):
                    if s.runs():
                        after(pe, s_sT, s.k + 1)
                        after(pe, s_x1, s.k)
                        for c in range(2):
                            t = nc.tensor.matmul(bank[5][:, c * P:(c + 1) * P], sT[s.odd][:, c * P:(c + 1) * P], w("cbd"),
                                                 start=True, stop=True)
                        t.then_inc(s_cp, 1)

                def x_turn(s):
                    if s.runs():
                        after(pe, s_xd[s.odd], uses(s))
                        after(pe, s_sT, s.k)
                        for c in range(2):
                            t = nc.tensor.transpose(bank[6][:, c * P:(c + 1) * P], xd[s.odd][:, c * P:(c + 1) * P], v.ident)
                        t.then_inc(s_xp, 1)

                def body(s):
                    centre_rows(s.back(3))
                    message_turn(nc, pe, s, bank, msg, v, s_msg, s_run, s_fp)
                    variance(nc, pe, s.back(1), bank, w, a, s_sq, s_ln, s_var)
                    centre_halves(nc, pe, s, bank, w, run, s_run, s_u, s_h)
                    x_turn(s.back(1))
                run_steps(pe, body, 3)

            @block.scalar
            def _(act):
                act.preload_act_table_set("natural_log_exp_and_others")

                def final_squares(s):
                    if s.runs():
                        after(act, s_cp, s.k + 1)
                        after(act, s_red, s.k)
                        nc.scalar.activation(sqf[:, :], bank[5][:, 0:256], ACT.Square).then_inc(s_fq, 1)

                def body(s):
                    squares(nc, act, s.back(1), bank, a, v.b2c, s_h, s_y, s_sq)
                    elu_exp(nc, act, s.back(2), a, b, vec(G2), vec(BE2), s_u, s_e)
                    final_squares(s.back(3))
                    final_log(nc, act, s.back(3), ssum, logs, vec(EPS), s_red, s_sf, s_lf)
                    final_exp(nc, act, s.back(3), logs, scale, s_lf, s_x1, s_sf)
                    norm_scale(nc, act, s.back(1), bank, b, vec(EPS), s_g, s_e, s_var, s_ln, s_rs)
                run_steps(act, body, 3)

            @block.vector
            def _(dve):
                def messages(s):
                    if s.runs():
                        after(dve, s_msg, s.k - 1)
                        nc.vector.tensor_tensor(
                            both[s.odd][:, :, :, :].rearrange("p t n c -> p (t n) c"),
                            v.xw[:, bass.ds(4 * s.k, 4), :].rearrange("p t (n c) -> p (t n) c", c=C),
                            v.att[:, bass.ds(4 * s.k, 4), 0:2].unsqueeze(3).to_broadcast([P, 4, 2, C]), ALU.mult
                        ).then_inc(s_both, 1)

                def rows(s):
                    if s.runs():
                        after(dve, s_sf, s.k + 1)
                        after(dve, s_x1r, s.k - 1)
                        after(dve, s_sc[s.odd], 64 * s.half)
                        for c in range(2):
                            z = nc.vector.tensor_tensor(
                                xrow[s.odd][:, c::2, :], bank[5][:, c * P:(c + 1) * P].rearrange("p (h f) -> p h f", h=2),
                                scale[:, 2 * c:2 * c + 2].unsqueeze(2).to_broadcast([P, 2, C]), ALU.mult)
                        z.then_inc(s_x1, 1)

                def keep_rows(s):
                    if s.runs():
                        after(dve, s_x1, s.k + 1)
                        nc.vector.tensor_copy(v.x1r[:, bass.ds(4 * s.k, 4), :], xrow[s.odd][:, :, :]).then_inc(s_x1r, 1)

                def residual(s):
                    if s.runs():
                        after(dve, s_y, s.k + 1)
                        after(dve, s_xp, s.k + 1)
                        after(dve, s_cp, s.k - 1)
                        nc.vector.tensor_tensor(sT[s.odd][:, :], zT[s.odd][:, :], bank[6][:, 0:256], ALU.add).then_inc(s_sT, 1)

                def body(s):
                    messages(s)
                    message_sum(nc, dve, s, both, msg, s_both, s_fp, s_msg)
                    elu_line(nc, dve, s.back(2), b, g, vec(G2), v.be2p, s_u, s_y, s_g)
                    elu_rows(nc, dve, s.back(2), a, g, zT, s_e, s_g, s_y, s_sT)
                    square_sums(nc, dve, s.back(3), sqf, ssum, s_fq, s_lf, s_red)
                    segment_scan(nc, dve, s, bank, keep, run, s_keep, s_fp, s_h, s_run)
                    residual(s.back(2))
                    rows(s.back(3))
                    norm_apply(nc, dve, s.back(1), bank, b, v.b2c, s_rs, s_u)
                    keep_rows(s.back(3))
                run_steps(dve, body, 3)


def square_sums(nc, dve, s, sqf, ssum, s_fq, s_lf, s_red):
    if s.runs():
        after(dve, s_fq, s.k + 1)
        after(dve, s_lf, s.k)
        nc.vector.tensor_reduce(ssum[:, :], sqf[:, :].rearrange("p (t f) -> p t f", f=C), AX.X, ALU.add).then_inc(s_red, 1)


def final_log(nc, act, s, ssum, logs, eps, s_red, s_sf, s_lf):
    if s.runs():
        after(act, s_red, s.k + 1)
        after(act, s_sf, s.k)
        nc.scalar.activation(logs[:, :], ssum[:, :], ACT.Ln, bias=eps, scale=1.0 / C).then_inc(s_lf, 1)


def final_exp(nc, act, s, logs, scale, s_lf, s_done, s_sf):
    if s.runs():
        after(act, s_lf, s.k + 1)
        after(act, s_done, s.k)
        nc.scalar.activation(scale[:, :], logs[:, :], ACT.Exp, scale=-0.5).then_inc(s_sf, 1)


def aggregate3(nc, sb0, sem, bank, w, vec, v, s_reviews):
    ph = ExitStack()

    def sb(name, shape, dt=F32):
        return sb0(name + "_a3", shape, dt, ph)

    with ph:
        rv = [sb(f"rv{h}", [P, 4, C]) for h in range(2)]
        rvT = [sb(f"rvT{h}", [P, 256]) for h in range(2)]
        gate = [sb(f"gate{h}", [P, 4, 2]) for h in range(2)]
        gx = [sb(f"gx{h}", [P, 4, C]) for h in range(2)]
        mx = [sb(f"mx{h}", [P, 4, C]) for h in range(2)]
        mr = [sb(f"mr{h}", [P, 4, C]) for h in range(2)]
        msg = [sb(f"msg{h}", [P, 4, C]) for h in range(2)]
        keep = [sb(f"keep{h}", [C, 512]) for h in range(2)]
        run = [sb(f"run{h}", [C, 512]) for h in range(2)]
        hc = [sb(f"hc{h}", [P, 4, C]) for h in range(2)]
        sqf = sb("sqf", [P, 256])
        ssum = sb("ssum", [P, 4])
        logs = sb("logs", [P, 4])
        scale = sb("scale", [P, 4])
        orow = [sb(f"orow{h}", [P, 4, C]) for h in range(2)]
        isrc = [sb(f"isrc{h}", [P, 4], I32) for h in range(2)]
        ilast = [sb(f"ilast{h}", [P, 4], I32) for h in range(2)]
        s_keep, s_il, s_is, s_ga, s_sc, s_rv = ([sem(f"{n}{h}") for h in range(2)] for n in (
            "s_keep", "s_il", "s_is", "s_ga", "s_sc", "s_rv"))
        (s_rp, s_rT, s_gp, s_ge, s_g1, s_g2, s_g3, s_gate, s_mr, s_mx, s_msg, s_fp, s_run, s_hp, s_hc, s_s, s_fq, s_red,
         s_lf, s_sf, s_o) = [sem(n) for n in (
             "s_rp s_rT s_gp s_ge s_g1 s_g2 s_g3 s_gate s_mr s_mx s_msg s_fp s_run s_hp s_hc s_s s_fq s_red "
             "s_lf s_sf s_o").split()]

        with nc.Block() as block:
            @block.sync
            def _(sp):
                def load(s):
                    if s.runs():
                        after_apart(sp, s_ga[s.odd], 64 * s.half, v.s_passed)
                        sp.dma_start(isrc[s.odd][:, :], v.srci[:, bass.ds(4 * s.k, 4)]).then_inc(s_is[s.odd], 16)
                        after_apart(sp, s_rp, s.k - 1, v.s_passed)
                        sp.dma_start(rv[s.odd][:, :, :], v.ea_s.rearrange("(t p) f -> t p f", p=P)[bass.ds(4 * s.k, 4)
                                     ].rearrange("t p f -> p t f")).then_inc(s_rv[s.odd], 16)
                    e = s.back(1)
                    if e.runs():
                        after_apart(sp, s_run, e.k - 1, v.s_passed)
                        sp.dma_start(keep[e.odd][:, :], v.same_d[bass.ds(512 * e.k, 512)].unsqueeze(0).to_broadcast([C, 512])
                                     ).then_inc(s_keep[e.odd], 16)

                def load_last(s):
                    if s.runs():
                        after_apart(sp, s_sc[s.odd], 64 * s.half, v.s_passed)
                        sp.dma_start(ilast[s.odd][:, :], v.lasti[:, bass.ds(4 * s.k, 4)]).then_inc(s_il[s.odd], 16)

                def body(s):
                    load(s.back(-1))
                    load_last(s.back(1))
                sp.wait_ge(s_reviews, 16)
                load(step(0))
                run_steps(sp, body, 2)

            @block.gpsimd
            def _(pool):
                def get(s):
                    if s.runs():
                        after_apart(pool, s_is[s.odd], uses(s), v.s_passed)
                        after_apart(pool, s_mx, s.k - 1, v.s_passed)
                        for t in range(4):
                            pool.indirect_dma_start(gx[s.odd][:, t, :], None, v.x1_table,
                                                    bass.IndirectOffsetOnAxis(ap=isrc[s.odd][:, t:t + 1], axis=0)
                                                    ).then_inc(s_ga[s.odd], 16)

                def put(s):
                    if s.runs():
                        after_apart(pool, s_il[s.odd], uses(s), v.s_passed)
                        after_apart(pool, s_o, s.k + 1, v.s_passed)
                        for t in range(4):
                            pool.indirect_dma_start(v.out, bass.IndirectOffsetOnAxis(ap=ilast[s.odd][:, t:t + 1], axis=0),
                                                    orow[s.odd][:, t, :], None, bounds_check=NP - 1, oob_is_err=False
                                                    ).then_inc(s_sc[s.odd], 16)

                def body(s):
                    get(s), put(s.back(2))
                run_steps(pool, body, 2)
                pool.wait_ge(s_sc[0], 64 * (STEPS // 2 + 1))
                pool.wait_ge(s_sc[1], 64 * (STEPS // 2))

            @block.tensor
            def _(pe):
                def review_turn(s):
                    if s.runs():
                        after(pe, s_rv[s.odd], uses(s))
                        after(pe, s_rT, s.k)
                        for c in range(2):
                            t = nc.tensor.transpose(bank[6][:, c * P:(c + 1) * P],
                                                    rv[s.odd][:, 2 * c:2 * c + 2, :].rearrange("p t f -> p (t f)"), v.ident)
                        t.then_inc(s_rp, 1)

                def reviews(s):
                    if s.runs():
                        after(pe, s_rT, s.k + 1)
                        after(pe, s_mr, s.k - 1)
                        for c in range(2):
                            t = nc.tensor.matmul(bank[2 + s.odd][:, c * 132:(c + 1) * 132], rvT[s.odd][:, c * P:(c + 1) * P],
                                                 w("rev"), start=True, stop=True)
                        t.then_inc(s_gp, 1)

                def sum_rows(s):
                    if s.runs():
                        after(pe, s_run, s.k + 1)
                        after(pe, s_hc, s.k)
                        for t in range(4):
                            z = nc.tensor.matmul(bank[5][:, t * C:(t + 1) * C], run[s.odd][:, t * P:(t + 1) * P],
                                                 w("cbd", C)[:, 0:C], start=True, stop=True)
                        z.then_inc(s_hp, 1)

                def body(s):
                    review_turn(s)
                    message_turn(nc, pe, s.back(1), bank, msg, v, s_msg, s_run, s_fp)
                    reviews(s)
                    sum_rows(s.back(1))
                run_steps(pe, body, 1)

            @block.scalar
            def _(act):
                act.preload_act_table_set("natural_log_exp_and_others")

                def review_copy(s):
                    if s.runs():
                        after(act, s_rp, s.k + 1)
                        after(act, s_gp, s.k - 1)
                        nc.scalar.activation(rvT[s.odd][:, :], bank[6][:, 0:256], ACT.Copy).then_inc(s_rT, 1)

                def gate_exp(s):
                    if s.runs():
                        after(act, s_gp, s.k + 1)
                        after(act, s_mr, s.k - 1)
                        after(act, s_mx, s.k - 1)
                        nc.scalar.activation(gate[s.odd][:, :, :], bank[2 + s.odd][:, 0:264].rearrange(
                            "p (t n) -> p t n", n=66)[:, :, C:C + 2], ACT.Exp, scale=-1.0).then_inc(s_ge, 1)

                def final_squares(s):
                    if s.runs():
                        after(act, s_s, s.k + 1)
                        after(act, s_red, s.k)
                        nc.scalar.activation(sqf[:, :], hc[s.odd][:, :, :].rearrange("p t f -> p (t f)"), ACT.Square
                                             ).then_inc(s_fq, 1)

                def body(s):
                    review_copy(s)
                    gate_exp(s)
                    final_squares(s.back(1))
                    final_log(nc, act, s.back(1), ssum, logs, vec(EPS), s_red, s_sf, s_lf)
                    final_exp(nc, act, s.back(1), logs, scale, s_lf, s_o, s_sf)
                run_steps(act, body, 1)

            @block.vector
            def _(dve):
                def gates(s):
                    if s.runs():
                        g = gate[s.odd]
                        cj = v.cjp[:, bass.ds(4 * s.k, 4)]
                        after(dve, s_ge, s.k + 1)
                        nc.vector.tensor_scalar(g[:, :, :], g[:, :, :], 1.0, None, ALU.add).then_inc(s_g1, 1)
                        after(dve, s_g1, s.k + 1)
                        nc.vector.reciprocal(g[:, :, :], g[:, :, :]).then_inc(s_g2, 1)
                        after(dve, s_g2, s.k + 1)
                        nc.vector.tensor_tensor(g[:, :, 1], g[:, :, 1], v.ewp[:, bass.ds(4 * s.k, 4)], ALU.mult).then_inc(s_g3, 1)
                        after(dve, s_g3, s.k + 1)
                        nc.vector.tensor_tensor(g[:, :, :], g[:, :, :], cj.unsqueeze(2).to_broadcast([P, 4, 2]), ALU.mult
                                                ).then_inc(s_gate, 1)

                def gated_reviews(s):
                    if s.runs():
                        after(dve, s_gate, s.k + 1)
                        after(dve, s_msg, s.k - 1)
                        nc.vector.tensor_tensor(mr[s.odd][:, :, :], bank[2 + s.odd][:, 0:264].rearrange(
                            "p (t n) -> p t n", n=66)[:, :, 0:C], gate[s.odd][:, :, 1:2].to_broadcast([P, 4, C]), ALU.mult
                        ).then_inc(s_mr, 1)

                def gated_sources(s):
                    if s.runs():
                        after(dve, s_ga[s.odd], 64 * s.half + 64)
                        nc.vector.tensor_tensor(mx[s.odd][:, :, :], gx[s.odd][:, :, :],
                                                gate[s.odd][:, :, 0:1].to_broadcast([P, 4, C]), ALU.mult
                                                ).then_inc(s_mx, 1)

                def messages(s):
                    if s.runs():
                        after(dve, s_mx, s.k + 1)
                        after(dve, s_fp, s.k - 1)
                        nc.vector.tensor_tensor(msg[s.odd][:, :, :], mx[s.odd][:, :, :], mr[s.odd][:, :, :], ALU.add
                                                ).then_inc(s_msg, 1)

                def sums(s):
                    if s.runs():
                        after(dve, s_hp, s.k + 1)
                        after(dve, s_o, s.k - 1)
                        nc.vector.tensor_tensor(hc[s.odd][:, :, :], bank[5][:, 0:256].rearrange("p (t f) -> p t f", f=C),
                                                v.cip[:, bass.ds(4 * s.k, 4)].unsqueeze(2).to_broadcast([P, 4, C]), ALU.mult
                                                ).then_inc(s_hc, 1)
                        after(dve, s_hc, s.k + 1)
                        nc.vector.tensor_tensor(hc[s.odd][:, :, :], hc[s.odd][:, :, :], v.x1r[:, bass.ds(4 * s.k, 4), :], ALU.add
                                                ).then_inc(s_s, 1)

                def rows(s):
                    if s.runs():
                        after(dve, s_sf, s.k + 1)
                        after(dve, s_sc[s.odd], 64 * s.half)
                        nc.vector.tensor_tensor(orow[s.odd][:, :, :], hc[s.odd][:, :, :],
                                                scale[:, :].unsqueeze(2).to_broadcast([P, 4, C]), ALU.mult).then_inc(s_o, 1)

                def body(s):
                    segment_scan(nc, dve, s.back(1), bank, keep, run, s_keep, s_fp, s_hp, s_run)
                    gates(s)
                    gated_reviews(s)
                    sums(s.back(1))
                    square_sums(nc, dve, s.back(1), sqf, ssum, s_fq, s_lf, s_red)
                    gated_sources(s)
                    messages(s)
                    rows(s.back(1))
                run_steps(dve, body, 1)


def kernel(x, src, dst, edge_attr_64, edge_weight, node_vec1, node_vec1_n2, L0_gnn_W1, L0_gnn_a1_src, L0_gnn_a1_dst,
           L0_gnn_b1, L0_gnn_W2, L0_gnn_a2_src, L0_gnn_a2_dst, L0_gnn_b2, L0_gnn_ln1_g, L0_gnn_ln1_b, L0_gnn_ln2_g,
           L0_gnn_ln2_b, L1_gnn_prob_w, L1_gnn_review_score_w, L1_gnn_review_w):
    import numpy as np
    import concourse.bacc as bacc
    from concourse.bass_utils import run_bass_kernel_spmd

    f32, i32 = np.float32, np.int32
    xp = np.zeros((NP, C), f32)
    xp[:N] = x
    xp = np.ascontiguousarray(xp.reshape(NP // UNIT, P, CH // 2, 2, C).transpose(0, 3, 4, 2, 1)).reshape(NP // UNIT, P, 512)
    xs = np.zeros((NP, ROW), f32)
    xs[:N, 0:1] = node_vec1
    xs[:N, 1:ROW] = x
    xt = np.zeros((NP, ROW), f32)
    xt[:N, 0:C] = x
    xt[:N, C:ROW] = node_vec1_n2
    srcp = np.full((EP,), N, i32)
    srcp[:E] = src
    dstp = np.full((EP + 2,), N, i32)
    dstp[0] = -1
    dstp[1:E + 1] = dst
    ewp = np.zeros((EP,), f32)
    ewp[:E] = edge_weight
    eap = np.zeros((EP, C), f32)
    eap[:E] = edge_attr_64

    wts = np.zeros((P, WIDTH), f32)

    def block(name):
        a, b = COLS[name]
        return wts[:, a:b]

    def twice(to, m):
        n = to.shape[1] // 2
        to[0:C, 0:m.shape[1]] = m
        to[C:P, n:n + m.shape[1]] = m

    centre = (np.eye(C) - 1.0 / C).astype(f32)
    block("ident")[:, :] = np.eye(P, dtype=f32)
    twice(block("cbd"), centre)
    twice(block("jbd"), np.full((C, C), 1.0 / C, f32))
    block("clo")[0:C, 0:C] = centre
    block("chi")[0:C, C:P] = centre
    W1, W2 = np.asarray(L0_gnn_W1), np.asarray(L0_gnn_W2)
    twice(block("w1t"), W1.T)
    twice(block("w1"), W1)
    twice(block("w2t"), W2.T)
    twice(block("w2"), W2)
    per = C // HEADS
    for h in range(HEADS):
        rows = slice(h * per, (h + 1) * per)
        low = slice(C + h * per, C + (h + 1) * per)
        block("al1")[rows, h] = L0_gnn_a1_src[h]
        block("al1")[low, h] = L0_gnn_a1_dst[h]
        block("al1")[low, HEADS + h] = L0_gnn_a1_src[h]
        block("al2")[low, HEADS + h] = L0_gnn_a1_dst[h]
    twice(block("sel2"), np.concatenate([np.eye(C, dtype=f32), np.asarray(L0_gnn_a2_src).T, np.asarray(L0_gnn_a2_dst).T], 1))
    twice(block("rev"), np.concatenate([np.asarray(L1_gnn_review_w).T, np.asarray(L1_gnn_prob_w).T,
                                        np.asarray(L1_gnn_review_score_w).T], 1))
    for i, m in ((B1, L0_gnn_b1), (B2, L0_gnn_b2), (G1, L0_gnn_ln1_g), (BE1, L0_gnn_ln1_b), (G2, L0_gnn_ln2_g),
                 (BE2, L0_gnn_ln2_b)):
        block("vec")[0:C, i] = m
        block("vec")[C:P, i] = m
    block("vec")[:, ONE] = 1.0
    block("vec")[:, EPS] = LN_EPS
    block("vec")[:, EPS2] = LN_EPS * LN_EPS

    nc = bacc.Bacc("TRN2", target_bir_lowering=False, num_devices=1)
    arrays = {"x": xp, "xs": xs, "xt": xt, "src": srcp, "dst": dstp, "ew": ewp, "ea": eap, "wts_in": wts}
    args = [nc.dram_tensor(n, a.shape, mybir.dt.from_np(a.dtype), kind="ExternalInput").ap() for n, a in arrays.items()]
    out = nc.dram_tensor("out", (NP, C), F32, kind="ExternalOutput").ap()
    gnn_program(nc, *args, out)
    r = run_bass_kernel_spmd(nc, [arrays], core_ids=[0])
    return r.results[0]["out"][:N]
```
